# Optimizing a Trainium2 kernel written in Bass

```python
import numpy as np
import jax
import jax.numpy as jnp

def _softmax(x, axis=-1):
    return jax.nn.softmax(x, axis=axis)

def _gelu(x):
    return jax.nn.gelu(x, approximate=True)

def _silu(x):
    return jax.nn.silu(x)

def _sigmoid(x):
    return jax.nn.sigmoid(x)

def _layernorm(x, axis=-1, eps=1e-05):
    m = jnp.mean(x, axis=axis, keepdims=True)
    v = jnp.var(x, axis=axis, keepdims=True)
    return (x - m) / jnp.sqrt(v + eps)

def _scatter_add(tgt, idx, src, axis=0):
    return tgt.at[idx].add(src)

def _segment_sum(src, seg, n):
    return jax.ops.segment_sum(src, seg, n)
kernel_name = 'mk_xattn_ffn_d1_seqx_r4_6440da'

def setup_inputs(seed: int=0):
    np.random.seed(seed)
    _w = jnp.asarray

    def _rec_inputs():
        import jax
        import jax.numpy as jnp
        _rk = jax.random.key(seed)
        x = -0.0003929 + 0.9999 * jax.random.normal(jax.random.fold_in(_rk, 1), (4, 1024, 256), jnp.float32)
        _lenS = 1024 - jax.random.randint(jax.random.fold_in(_rk, 7), (4,), 0, max(1, 1024 // 4) + 1, jnp.int32)
        _lenS2 = 64 - jax.random.randint(jax.random.fold_in(_rk, 8), (4,), 0, max(1, 64 // 4) + 1, jnp.int32)
        _ctx_768P = jax.random.normal(jax.random.fold_in(_rk, 11), (4, 16, 192), jnp.float32)
        _ctx_768c = jax.random.dirichlet(jax.random.fold_in(_rk, 511), 0.3 * jnp.ones((16,), jnp.float32), (4, 64))
        _ctx_768t = jnp.einsum('bsk,bkd->bsd', _ctx_768c, _ctx_768P)
        _ctx_768t = _ctx_768t * jax.lax.rsqrt(jnp.mean(jnp.square(_ctx_768t)) + 1e-12) * 0.953939
        ctx_768 = -7.36909e-05 + 0.999899 * (_ctx_768t + 0.3 * jax.random.normal(jax.random.fold_in(_rk, 611), (4, 64, 192), jnp.float32))
        return (x, ctx_768)
    x, ctx_768 = _rec_inputs()

    def _L0_xattn_setup():
        import jax, jax.numpy as jnp
        import numpy as np
        IMG_DIM, TXT_DIM, HID = (256, 192, 256)
        B, LQ, LK = (8, 512, 512)
        key = jax.random.key(seed)
        ks = jax.random.split(key, 8)
        s_img = 1.0 / np.sqrt(IMG_DIM)
        s_txt = 1.0 / np.sqrt(TXT_DIM)
        return {'image_features': jax.random.normal(ks[0], (B, LQ, IMG_DIM), jnp.float32), 'text_features': jax.random.normal(ks[1], (B, LK, TXT_DIM), jnp.float32), 'Wq': jax.random.uniform(ks[2], (IMG_DIM, HID), jnp.float32, -s_img, s_img), 'bq': jax.random.uniform(ks[3], (HID,), jnp.float32, -s_img, s_img), 'Wk': jax.random.uniform(ks[4], (TXT_DIM, HID), jnp.float32, -s_txt, s_txt), 'bk': jax.random.uniform(ks[5], (HID,), jnp.float32, -s_txt, s_txt), 'Wv': jax.random.uniform(ks[6], (TXT_DIM, HID), jnp.float32, -s_txt, s_txt), 'bv': jax.random.uniform(ks[7], (HID,), jnp.float32, -s_txt, s_txt)}
    _L0_xattn_all = _L0_xattn_setup()
    _L0_xattn_in = {k: v for k, v in _L0_xattn_all.items() if k in ('Wq', 'bq', 'Wk', 'bk', 'Wv', 'bv')}
    del _L0_xattn_all

    def _L0_ffn_setup():
        import jax, jax.numpy as jnp
        import numpy as np
        E = 8
        K = 2
        CAP_RATIO = 1.05
        key = jax.random.key(seed)
        ks = jax.random.split(key, 4)
        B, S, D, H = (2, 512, 256, 1024)
        x = jax.random.normal(ks[0], (B, S, D), jnp.float32)
        Wg = jax.random.normal(ks[1], (E, D), jnp.float32) * 0.02
        W1 = jax.random.normal(ks[2], (E, D, H), jnp.float32) * 0.02
        b1 = jnp.zeros((E, H), jnp.float32)
        W2 = jax.random.normal(ks[3], (E, H, D), jnp.float32) * 0.02
        b2 = jnp.zeros((E, D), jnp.float32)
        return {'x': x, 'Wg': Wg, 'W1': W1, 'b1': b1, 'W2': W2, 'b2': b2}
    _L0_ffn_all = _L0_ffn_setup()
    _L0_ffn_in = {k: v for k, v in _L0_ffn_all.items() if k in ('Wg', 'W1', 'b1', 'W2', 'b2')}
    del _L0_ffn_all
    return {'x': x, 'ctx_768': ctx_768, 'L0_xattn_Wq': _L0_xattn_in['Wq'], 'L0_xattn_bq': _L0_xattn_in['bq'], 'L0_xattn_Wk': _L0_xattn_in['Wk'], 'L0_xattn_bk': _L0_xattn_in['bk'], 'L0_xattn_Wv': _L0_xattn_in['Wv'], 'L0_xattn_bv': _L0_xattn_in['bv'], 'L0_ffn_Wg': _L0_ffn_in['Wg'], 'L0_ffn_W1': _L0_ffn_in['W1'], 'L0_ffn_b1': _L0_ffn_in['b1'], 'L0_ffn_W2': _L0_ffn_in['W2'], 'L0_ffn_b2': _L0_ffn_in['b2']}

def reference(x, ctx_768, L0_xattn_Wq, L0_xattn_bq, L0_xattn_Wk, L0_xattn_bk, L0_xattn_Wv, L0_xattn_bv, L0_ffn_Wg, L0_ffn_W1, L0_ffn_b1, L0_ffn_W2, L0_ffn_b2):
    import jax
    import jax.numpy as jnp

    def _L0_xattn_ref(image_features, text_features, Wq, bq, Wk, bk, Wv, bv):
        import jax, jax.numpy as jnp
        import numpy as np
        IMG_DIM, TXT_DIM, HID = (256, 192, 256)
        B, LQ, LK = (8, 512, 512)
        query = jnp.einsum('bqi,ih->bqh', image_features, Wq) + bq
        key = jnp.einsum('bkt,th->bkh', text_features, Wk) + bk
        value = jnp.einsum('bkt,th->bkh', text_features, Wv) + bv
        scale = 1.0 / jnp.sqrt(jnp.asarray(HID, query.dtype))
        scores = jnp.einsum('bqh,bkh->bqk', query, key) * scale
        weights = jax.nn.softmax(scores, axis=-1)
        attended = jnp.einsum('bqk,bkh->bqh', weights, value)
        return attended

    def _L0_ffn_ref(x, Wg, W1, b1, W2, b2):
        import jax, jax.numpy as jnp
        import numpy as np
        E = 8
        K = 2
        CAP_RATIO = 1.05
        B, S, D = x.shape
        T = B * S
        xf = x.reshape(T, D)
        gates = jax.nn.softmax(xf @ Wg.T, axis=-1)
        topw, topi = jax.lax.top_k(gates, K)
        C = int(round(K * T * CAP_RATIO / E))
        e_ord = topi.T.reshape(-1)
        tok_ord = jnp.tile(jnp.arange(T), K)
        oh = jax.nn.one_hot(e_ord, E, dtype=jnp.int32)
        cnt = jnp.take_along_axis(jnp.cumsum(oh, 0) - oh, e_ord[:, None], 1)[:, 0]
        within = cnt < C
        pos = jnp.where(within, cnt, C)
        x_disp = xf[tok_ord]
        buf = jnp.zeros((E, C + 1, D), xf.dtype).at[e_ord, pos].add(x_disp)[:, :C]
        h = jax.nn.gelu(jnp.einsum('ecd,edh->ech', buf, W1) + b1[:, None, :], approximate=False)
        y = jnp.einsum('ech,ehd->ecd', h, W2) + b2[:, None, :]
        y_ord = y[e_ord, jnp.minimum(pos, C - 1)] * within[:, None].astype(y.dtype)
        y_tk = y_ord.reshape(K, T, D).transpose(1, 0, 2)
        cw = topw * within.reshape(K, T).T.astype(topw.dtype)
        out = jnp.einsum('tk,tkd->td', cw, y_tk)
        return out.reshape(B, S, D)
    x = x + _L0_xattn_ref(_layernorm(x, axis=-1), ctx_768, L0_xattn_Wq, L0_xattn_bq, L0_xattn_Wk, L0_xattn_bk, L0_xattn_Wv, L0_xattn_bv)
    x = x + _L0_ffn_ref(_layernorm(x, axis=-1), L0_ffn_Wg, L0_ffn_W1, L0_ffn_b1, L0_ffn_W2, L0_ffn_b2)
    return x

_drawn_inputs = setup_inputs


def setup_inputs(seed=0):
    import zlib

    import numpy as np

    out = dict(_drawn_inputs(seed))
    spreads = {'L0_ffn_b1': (0.0, 0.8), 'L0_ffn_b2': (0.0, 0.332)}
    factors = {'L0_xattn_bq': 8.0, 'L0_xattn_bk': 8.0}
    for name, (base, spread) in spreads.items():
        noise = np.random.default_rng([zlib.crc32(name.encode()), seed]).standard_normal(out[name].shape)
        drawn = base * np.exp(spread * noise) if base else spread * noise
        out[name] = jnp.asarray(drawn.astype(out[name].dtype))
    for name, factor in factors.items():
        out[name] = (out[name] * factor).astype(out[name].dtype)
    return out
```

```python
from contextlib import ExitStack

import concourse.bass as bass
from concourse import mybir

P = 128
F32 = mybir.dt.float32
F32R = mybir.dt.float32r
BF16 = mybir.dt.bfloat16
I32 = mybir.dt.int32
ALU = mybir.AluOpType
ACT = mybir.ActivationFunctionType
AX = mybir.AxisListType
EPS = 1e-5
ROUNDER = 12582912.0
TOP_K = 2
CAP_RATIO = 1.05


def upto(value):
    return max(value, 0) if isinstance(value, int) else value


def xattn_moe(nc, x, ctx_in, Wq, bq, Wk, bk, Wv, bv, Wg, W1, b1, W2, b2, out):
    B, S, D = x.shape
    T = B * S
    KEYS, CD = ctx_in.shape[1:]
    E, _, H = W1.shape
    C = int(round(TOP_K * T * CAP_RATIO / E))
    TILES = T // P
    PAIRS = TILES // 2
    PB = PAIRS // B
    KD = D // P
    HC = H // P
    CR = CD - P
    ST = -(-C // P)
    UT = 3
    UE = ST // UT
    LAST = (C - (ST - 1) * P + 1) // 2 * 2
    SLOTS = ST * P
    UNITS = E * UE
    BODY = 2 * UE
    ROW = D + E
    NT = E * ST
    assert KD == 2 and PB == 4 and ST % UT == 0 and UE == 3 and KEYS == 64 and P < CD <= 2 * P and TILES % 2 == 0

    with ExitStack() as stack:
        def sb(name, shape, dt=F32):
            return stack.enter_context(nc.sbuf_tensor(name, shape, dt))

        def sem(name):
            return stack.enter_context(nc.semaphore(name))

        rows_dram = nc.dram_tensor("rows_scratch", (T + P, ROW), F32).ap()

        bank = [stack.enter_context(nc.psum_tensor(f"bank{i}", [P, 512], F32)) for i in range(8)]
        ps_xT, ps_score, ps_pT, ps_att, ps_x2T, ps_logit = bank[0:6]
        ps_prefix, ps_total, ps_table = bank[5], bank[6], bank[7]
        ps_up, ps_turn, ps_y = bank[0:3], bank[3:5], bank[5:8]

        ident = sb("ident", [P, P])
        zeros = sb("zeros", [P, ROW])
        b1_sb = sb("b1_sb", [E * HC, P])
        b1T = sb("b1T", [P, E * HC])
        slot_token = sb("slot_token", [P, NT], I32)
        unit_token = sb("unit_token", [P, BODY, UT], I32)
        w1_raw = sb("w1_raw", [P, KD, H])
        w2_raw = sb("w2_raw", [P, HC, D])
        w1_hi = [sb(f"w1_hi{i}", [P, KD, H], F32R) for i in range(2)]
        w1_lo = [sb(f"w1_lo{i}", [P, KD, H], F32R) for i in range(2)]
        w2_hi = [sb(f"w2_hi{i}", [P, HC, D], F32R) for i in range(2)]
        w2_lo = [sb(f"w2_lo{i}", [P, HC, D], F32R) for i in range(2)]
        b2_wide = sb("b2_wide", [P, 2, D])
        gathered = sb("gathered", [P, 3, UT, ROW])

        early = ExitStack()

        def tmp(name, shape, dt=F32):
            return early.enter_context(nc.sbuf_tensor(name, shape, dt))

        iota_slot = tmp("iota_slot", [P, P])
        iota_tile = tmp("iota_tile", [P, NT])
        iota_e8 = tmp("iota_e8", [P, TILES, E])
        token1 = tmp("token1", [P, TILES])
        trash = tmp("trash", [P, NT])
        before = tmp("before", [P, P], BF16)
        ones_bf = tmp("ones_bf", [P, P], BF16)
        ones = tmp("ones", [P, P])
        mean_w = tmp("mean_w", [P, P])
        minus_half = tmp("minus_half", [P, 2])
        scan_keep = tmp("scan_keep", [P, TOP_K * E, TILES])
        wq_sb = tmp("wq_sb", [P, KD, D])
        wk_sb = tmp("wk_sb", [P, 2, D])
        wv_sb = tmp("wv_sb", [P, 2, D])
        ctx_sb = tmp("ctx_sb", [P, 2, CD])
        ctxT = tmp("ctxT", [P, 2, B * KEYS])
        bq_sb = tmp("bq_sb", [P, KD])
        bk_sb = tmp("bk_sb", [P, KD])
        bq_wide = tmp("bq_wide", [P, KD, P])
        bv_sb = tmp("bv_sb", [KEYS, D])
        wqT = tmp("wqT", [P, KD, D])
        keyT = tmp("keyT", [P, KD, B * KEYS])
        a_raw = tmp("a_raw", [P, KD, B * KEYS])
        a_sb = tmp("a_sb", [P, KD, B * KEYS])
        c_sb = tmp("c_sb", [P, B * KEYS])
        v_sb = tmp("v_sb", [KEYS, B, D])
        wg_sb = tmp("wg_sb", [E, D])
        wgT = tmp("wgT", [P, KD, E])
        x_sb = tmp("x_sb", [P, 4, 2, D])
        xT = tmp("xT", [P, 2, KD, 2 * P])
        stat1 = tmp("stat1", [P, 2, 2, 6])
        mv1 = tmp("mv1", [P, 2, 2, 2])
        var1 = tmp("var1", [P, 2, 2])
        rstd1 = tmp("rstd1", [P, 2, 2])
        score = tmp("score", [P, 2, 2, KEYS])
        nmax = tmp("nmax", [P, 2, 2])
        prob = tmp("prob", [P, 2, 2, KEYS])
        psum_row = tmp("psum_row", [P, 2, 2])
        pinv = tmp("pinv", [P, 2, 2])
        pT = tmp("pT", [KEYS, 2, 2 * P])
        x1 = tmp("x1", [P, 2, 2, D])
        stat2 = tmp("stat2", [P, 2, 2, 6])
        mv2 = tmp("mv2", [P, 2, 2, 2])
        var2 = tmp("var2", [P, 2, 2])
        nmean2 = tmp("nmean2", [P, 2, 2])
        rstd2 = tmp("rstd2", [P, 2, 2])
        shift2 = tmp("shift2", [P, 2, 2])
        rows = tmp("rows", [P, 4, 2, ROW])
        x2T = tmp("x2T", [P, 2, KD, 2 * P])
        gmax = tmp("gmax", [P, 2, 2])
        gsub = tmp("gsub", [P, 2, 2, E])
        gexp = tmp("gexp", [P, 2, 2, E])
        gsum = tmp("gsum", [P, 2, 2])
        ginv = tmp("ginv", [P, 2, 2])
        gates = tmp("gates", [P, TILES, E])
        best = tmp("best", [P, TOP_K, TILES])
        same = tmp("same", [P, TILES, E])
        choice = tmp("choice", [P, TOP_K, TILES])
        hot = tmp("hot", [P, TOP_K, TILES, E], BF16)
        rest = tmp("rest", [P, TILES, E])
        running = tmp("running", [P, TOP_K * E, TILES])
        place = tmp("place", [P, TOP_K * E, TILES])
        picked = tmp("picked", [P, TOP_K * E, TILES])
        count = tmp("count", [P, TOP_K, TILES])
        over = tmp("over", [P, TOP_K, TILES])
        slot = tmp("slot", [P, TOP_K, TILES])
        tile_f = tmp("tile_f", [P, TOP_K, TILES])
        slot_lo = tmp("slot_lo", [P, TOP_K, TILES])
        tile_of = tmp("tile_of", [P, TOP_K, TILES])
        slot_hot = tmp("slot_hot", [P, 4, P])
        tile_hot = tmp("tile_hot", [P, 4, NT])
        table = tmp("table", [P, 2 * NT])
        table1 = tmp("table1", [P, NT])
        table2 = tmp("table2", [P, NT])
        table3 = tmp("table3", [P, NT])
        early.close()

        gate_of = sb("gate_of", [P, 3, UT])
        in_hi = [sb(f"in_hi{i}", [P, KD, UT * P], F32R) for i in range(2)]
        in_lo = [sb(f"in_lo{i}", [P, KD, UT * P], F32R) for i in range(2)]
        h_f32 = sb("h_f32", [P, 3, UT * P])
        h_hi = [sb(f"h_hi{i}", [P, HC, UT * P], F32R) for i in range(2)]
        h_lo = [sb(f"h_lo{i}", [P, HC, UT * P], F32R) for i in range(2)]
        y_sum = sb("y_sum", [P, UT, D])
        y_out = sb("y_out", [P, UT, D])

        attn_in, b1_in, wg_in = sem("attn_in"), sem("b1_in"), sem("wg_in")
        pad_stored = sem("pad_stored")
        consts = sem("consts")
        zeroed = sem("zeroed")
        prep_pe, prep_dve = sem("prep_pe"), sem("prep_dve")

        pool_waits, act_waits, dve_waits, pe_waits = sem("pool_waits"), sem("act_waits"), sem("dve_waits"), sem("pe_waits")

        x_in = [sem(f"x_in{i}") for i in range(4)]
        xT_made, xT_copied, scores_made, scores_read = sem("xT_made"), sem("xT_copied"), sem("scores_made"), sem("scores_read")
        stats1_made, mv1_made, var1_made, rstd1_made = sem("stats1_made"), sem("mv1_made"), sem("var1_made"), sem("rstd1_made")
        score_scaled = sem("score_scaled")
        probs_made, pT_made, pT_copied, att_made = sem("probs_made"), sem("pT_made"), sem("pT_copied"), sem("att_made")
        pinv_made, x1_made, stats2_made, mv2_made = sem("pinv_made"), sem("x1_made"), sem("stats2_made"), sem("mv2_made")
        var2_made, rstd2_made, shift2_made, rows_made = sem("var2_made"), sem("rstd2_made"), sem("shift2_made"), sem("rows_made")
        x1_stored = [sem(f"x1_stored{i}") for i in range(2)]
        rows_stored = [sem(f"rows_stored{i}") for i in range(4)]
        x2T_made, x2T_copied, logits_made = sem("x2T_made"), sem("x2T_copied"), sem("logits_made")
        gmax_made, gsub_made, gexp_made, gsum_made, ginv_made, gates_made, rows_gated = (
            sem("gmax_made"), sem("gsub_made"), sem("gexp_made"), sem("gsum_made"), sem("ginv_made"),
            sem("gates_made"), sem("rows_gated"))

        route = sem("route")
        counts_made = sem("counts_made")
        hot_made, hot_free = sem("hot_made"), sem("hot_free")
        table_made, slots_ready = sem("table_made"), sem("slots_ready")

        w1_in, w2_in = sem("w1_in"), sem("w2_in")
        b2_in = [sem("b2_in0"), sem("b2_in1")]
        w1_hi_made, w1_lo_made, w2_hi_made, w2_lo_made = sem("w1_hi_made"), sem("w1_lo_made"), sem("w2_hi_made"), sem("w2_lo_made")
        rows_in = [sem(f"rows_in{i}") for i in range(3)]
        unit_token_made, gate_copied = sem("unit_token_made"), sem("gate_copied")
        turned, in_hi_made, in_lo_made = sem("turned"), sem("in_hi_made"), sem("in_lo_made")
        up_made, gelu_made, h_hi_made, h_lo_made = sem("up_made"), sem("gelu_made"), sem("h_hi_made"), sem("h_lo_made")
        down_made, y_summed, y_ready, y_added = sem("down_made"), sem("y_summed"), sem("y_ready"), sem("y_added")

        x_pairs = x.rearrange("b s d -> (b s) d").rearrange("(n t p) d -> n p t d", t=2, p=P)
        out_pairs = out[0:T, :].rearrange("(n t p) d -> n p t d", t=2, p=P)
        rows_pairs = rows_dram[0:T, :].rearrange("(n t p) d -> n p t d", t=2, p=P)
        w1_view = W1.rearrange("e (k p) h -> e p k h", p=P)
        w2_view = W2.rearrange("e (c p) d -> e p c d", p=P)

        def one(view, i):
            if isinstance(i, int):
                return view[i]
            names = "abc"[:len(view.shape) - 1]
            return view[bass.ds(i, 1)].rearrange(f"o {' '.join(names)} -> (o {names[0]}) {' '.join(names[1:])}")

        def cols(ap, start, size):
            return ap[:, start:start + size] if isinstance(start, int) else ap[:, bass.ds(start, size)]

        def steps_of_part1(eng, step):
            for s in range(PB):
                step(0, s, [s - lag >= 0 for lag in range(4)])
            with eng.Fori(1, PAIRS // PB) as it:
                for j in range(PB):
                    step(it, j, [True] * 4)
            for s in range(PAIRS, PAIRS + 3):
                step(PAIRS // PB, s - PAIRS, [s - lag < PAIRS for lag in range(4)])

        def steps_of_part3(eng, step):
            with eng.Fori(0, UNITS // BODY - 1) as it:
                for u in range(BODY):
                    step(it, u, False)
            for u in range(BODY):
                step(UNITS // BODY - 1, u, True)

        def tile_rows(u, j):
            return LAST if u % UE == UE - 1 and j == UT - 1 else P

        def unit_cols(u):
            return (UT - 1) * P + tile_rows(u, UT - 1)

        block = stack.enter_context(nc.Block())

        @block.sync
        def _(sp):
            def load_x(pair, ring):
                sp.dma_start(x_sb[:, ring], one(x_pairs, pair)).then_inc(x_in[ring], 16)

            sp.dma_start(ctx_sb[:], ctx_in.rearrange("b k c -> (b k) c").rearrange("(n p) c -> p n c", p=P)).then_inc(attn_in, 16)
            for w, t in ((Wk, wk_sb), (Wv, wv_sb)):
                sp.dma_start(t[:, 0, :], w[0:P, :]).then_inc(attn_in, 16)
                sp.dma_start(t[0:CR, 1, :], w[P:CD, :]).then_inc(attn_in, 16)
            sp.dma_start(wq_sb[:], Wq.rearrange("(k p) h -> p k h", p=P)).then_inc(attn_in, 16)
            with nc.allow_non_contiguous_dma(reason="two columns of 128 biases"):
                sp.dma_start(bq_sb[:], bq.rearrange("(k p) -> p k", p=P)).then_inc(attn_in, 16)
                sp.dma_start(bk_sb[:], bk.rearrange("(k p) -> p k", p=P)).then_inc(attn_in, 16)
            sp.dma_start(bv_sb[:], bv.rearrange("(o d) -> o d", o=1).to_broadcast([KEYS, D])).then_inc(attn_in, 16)
            load_x(0, 0)
            load_x(1, 1)
            sp.dma_start(wg_sb[:], Wg).then_inc(wg_in, 16)
            sp.dma_start(b1_sb[:], b1.rearrange("e (c p) -> (e c) p", p=P)).then_inc(b1_in, 16)
            sp.wait_ge(zeroed, 1)
            sp.dma_start(rows_dram[T:T + P, :], zeros[:]).then_inc(pad_stored, 16)

            def load_w1(e):
                sp.dma_start(w1_raw[:], one(w1_view, e)).then_inc(w1_in, 16)

            def load_w2(e):
                sp.dma_start(w2_raw[:], one(w2_view, e)).then_inc(w2_in, 16)

            def load_b2(e, ring):
                sp.dma_start(b2_wide[:, ring], (b2[e:e + 1] if isinstance(e, int) else b2[bass.ds(e, 1)]).to_broadcast([P, D])).then_inc(b2_in[ring], 16)

            def step1(it, j, on):
                ahead = j + 2
                if on[0] and not (isinstance(it, int) and 4 * it + ahead >= PAIRS):
                    sp.wait_ge(x1_made, upto(4 * it + ahead - 3))
                    load_x(4 * it + ahead, ahead % 4)
                if on[1]:
                    sp.wait_ge(x1_made, 4 * it + j)
                    sp.dma_start(one(out_pairs, 4 * it + j - 1), x1[:, (j - 1) % 2]).then_inc(x1_stored[(j - 1) % 2], 16)
                if on[3]:
                    sp.wait_ge(rows_gated, upto(4 * it + j - 2))
                    sp.dma_start(one(rows_pairs, 4 * it + j - 3), rows[:, (j - 3) % 4]).then_inc(rows_stored[(j - 3) % 4], 16)

            for s in range(PB):
                step1(0, s, [s - lag >= 0 for lag in range(4)])
            with sp.Fori(1, PAIRS // PB - 1) as it:
                for j in range(PB):
                    step1(it, j, [True] * 4)
            for s in range(PAIRS - PB, PAIRS + 3):
                step1(s // PB, s % PB, [s - lag < PAIRS for lag in range(4)])

            load_w1(0)
            load_w2(0)
            load_b2(0, 0)

            def step3(it, u, last):
                e = 2 * it + u // UE
                if last and u >= UE:
                    return
                if u % UE == 0:
                    sp.wait_ge(w1_hi_made, 4 * e + 4)
                    sp.wait_ge(w1_lo_made, 4 * e + 4)
                    load_w1(e + 1)
                    sp.wait_ge(w2_hi_made, 4 * e + 4)
                    sp.wait_ge(w2_lo_made, 4 * e + 4)
                    load_w2(e + 1)
                    sp.wait_ge(y_summed, UT * UE * e + 1)
                    load_b2(e + 1, (u // UE + 1) % 2)

            steps_of_part3(sp, step3)
            sp.wait_ge(y_added, 16 * (UT * UNITS + 1))

        @block.gpsimd
        def _(pool):

            n = 0

            def const(ins):
                nonlocal n
                n += 1
                ins.then_inc(consts, 1)

            small = dict(allow_small_or_imprecise_dtypes=True)
            pool.wait_ge(zeroed, 2)
            pool.dma_start(out[T:T + P, :], zeros[:, 0:D]).then_inc(y_added, 16)
            const(pool.affine_select(out=ident[:], in_=ones[:], compare_op=ALU.is_equal, fill=0.0, base=0, pattern=[[-1, P]], channel_multiplier=1))
            const(pool.memset(minus_half[:], -0.5))
            const(pool.iota(iota_slot[:], [[1, P]], base=0, channel_multiplier=0, **small))
            const(pool.iota(iota_tile[:], [[1, NT]], base=0, channel_multiplier=0, **small))
            const(pool.iota(iota_e8[:], [[0, TILES], [1, E]], base=-E, channel_multiplier=0, **small))
            const(pool.iota(token1[:], [[P, TILES]], base=1, channel_multiplier=1, **small))
            const(pool.iota(trash[:], [[0, NT]], base=T + 1, channel_multiplier=1, **small))
            pool.wait_ge(zeroed, 3)
            const(pool.affine_select(out=before[:], in_=before[:], compare_op=ALU.is_ge, fill=0.0, base=0, pattern=[[-1, P]], channel_multiplier=1))
            pool.wait_ge(zeroed, 4)
            const(pool.affine_select(out=scan_keep[:], in_=scan_keep[:], compare_op=ALU.is_gt, fill=0.0, base=0, pattern=[[0, TOP_K * E], [1, TILES]], channel_multiplier=0))
            pool.wait_ge(consts, n)

            def step1(it, j, on):
                pair = 4 * it + j
                if on[0]:
                    r = j % 2
                    pool.wait_ge(mv1_made, pair + 1)
                    pool.wait_ge(score_scaled, upto(pair - 1))
                    pool.sem_inc(pool_waits, 1)
                    pool.tensor_scalar(var1[:, r], mv1[:, r, :, 1], 1.0, EPS, ALU.mult, ALU.add).then_inc(var1_made, 1)
                    pool.wait_ge(var1_made, pair + 1)
                    pool.tensor_tensor(rstd1[:, r], var1[:, r], minus_half[:], ALU.pow).then_inc(rstd1_made, 1)
                if on[1]:
                    r, ring = (j - 1) % 2, (j - 1) % 4
                    pool.wait_ge(mv2_made, pair)
                    pool.sem_inc(pool_waits, 1)
                    pool.tensor_scalar(var2[:, r], mv2[:, r, :, 1], 1.0, EPS, ALU.mult, ALU.add)
                    pool.tensor_scalar(nmean2[:, r], mv2[:, r, :, 0], -1.0, 0.0, ALU.mult, ALU.add).then_inc(var2_made, 1)
                    pool.wait_ge(var2_made, pair)
                    pool.tensor_tensor(rstd2[:, r], var2[:, r], minus_half[:], ALU.pow).then_inc(rstd2_made, 1)
                    pool.wait_ge(rstd2_made, pair)
                    pool.tensor_tensor(shift2[:, r], nmean2[:, r], rstd2[:, r], ALU.mult).then_inc(shift2_made, 1)
                    pool.wait_ge(shift2_made, pair)
                    pool.wait_ge(rows_stored[ring], upto(16 * (it + (j - 1) // 4)))
                    pool.sem_inc(pool_waits, 1)
                    for t in range(2):
                        ins = pool.tensor_scalar(rows[:, ring, t, 0:D], x1[:, r, t], rstd2[:, r, t:t + 1], shift2[:, r, t:t + 1], ALU.mult, ALU.add)
                    ins.then_inc(rows_made, 1)

            steps_of_part1(pool, step1)

            def w1_low(e, par):
                w1h, w1l, raw = (a[:].rearrange("p k (b h) -> p (k b) h", b=2) for a in (w1_hi[par], w1_lo[par], w1_raw))
                for b in range(4):
                    pool.wait_ge(w1_hi_made, 4 * e + b + 1)
                    pool.tensor_tensor(w1l[:, b], raw[:, b], w1h[:, b].bitcast(F32), ALU.subtract).then_inc(w1_lo_made, 1)

            def w2_low(e, par):
                w2h, w2l, raw = (a[:].rearrange("p (b c) d -> p b (c d)", b=4) for a in (w2_hi[par], w2_lo[par], w2_raw))
                for b in range(4):
                    pool.wait_ge(w2_hi_made, 4 * e + b + 1)
                    pool.tensor_tensor(w2l[:, b], raw[:, b], w2h[:, b].bitcast(F32), ALU.subtract).then_inc(w2_lo_made, 1)

            pool.wait_ge(w1_in, 16)
            w1_low(0, 0)
            pool.wait_ge(w2_in, 16)
            w2_low(0, 0)

            def gather(it, u):
                ring, index = u % 3, u % BODY
                unit = BODY * it + u
                pool.tensor_copy(unit_token[:, index], cols(slot_token, UT * unit, UT)).then_inc(unit_token_made, 1)
                pool.wait_ge(unit_token_made, unit + 1)
                pool.sem_inc(pool_waits, 1)
                for j in range(UT):
                    n_rows = tile_rows(u, j)
                    pool.indirect_dma_start(
                        gathered[0:n_rows, ring, j, :], None, rows_dram[:, :],
                        bass.IndirectOffsetOnAxis(ap=unit_token[0:n_rows, index, j:j + 1], axis=0),
                    ).then_inc(rows_in[ring], 16)

            for ring in range(4):
                pool.wait_ge(rows_stored[ring], 16 * PAIRS // 4)
            for ring in range(2):
                pool.wait_ge(x1_stored[ring], 16 * PAIRS // 2)
            pool.wait_ge(pad_stored, 16)
            pool.wait_ge(slots_ready, 1)
            for u in range(3):
                gather(0, u)

            def step3(it, u, last):
                unit = BODY * it + u
                e = 2 * it + u // UE
                par = (u // UE + 1) % 2
                if not last or u + 3 < BODY:
                    pool.wait_ge(turned, unit + 1)
                    pool.wait_ge(gate_copied, unit + 1)
                    gather(it, u + 3)
                if not last or u < UE:
                    if u % UE == 0:
                        w1_low(e + 1, par)
                    if u % UE == 1:
                        w2_low(e + 1, par)
                for j in range(UT):
                    n_rows, tile = tile_rows(u, j), UT * unit + j
                    pool.wait_ge(y_ready, tile + 2)
                    pool.wait_ge(y_added, 16 * (tile + 1))
                    pool.sem_inc(pool_waits, 1)
                    pool.indirect_dma_start(
                        out[:, :], bass.IndirectOffsetOnAxis(ap=unit_token[0:n_rows, u, j:j + 1], axis=0),
                        y_out[0:n_rows, j, :], None, compute_op=ALU.add,
                    ).then_inc(y_added, 16)

            steps_of_part3(pool, step3)

        @block.scalar
        def _(act):

            def step1(it, j, on):
                pair = 4 * it + j
                if on[1]:
                    r = (j - 1) % 2
                    act.wait_ge(score_scaled, pair)
                    act.wait_ge(pT_made, upto(pair - 2))
                    act.wait_ge(pinv_made, upto(pair - 2))
                    for t in range(2):
                        ins = act.activation(prob[:, r, t], score[:, r, t], ACT.Exp, bias=nmax[:, r, t:t + 1], accum_out=psum_row[:, r, t:t + 1])
                    ins.then_inc(probs_made, 1)
                if on[3]:
                    r = (j - 3) % 2
                    act.wait_ge(gsub_made, upto(pair - 2))
                    act.wait_ge(gates_made, upto(pair - 4))
                    act.activation(gexp[:, r], gsub[:, r], ACT.Exp).then_inc(gexp_made, 1)
                if on[0]:
                    r = j % 2
                    act.wait_ge(xT_made, pair + 1)
                    act.wait_ge(scores_made, upto(pair - 1))
                    act.copy(xT[:, r], ps_xT[:].rearrange("p (k t) -> p k t", k=KD)).then_inc(xT_copied, 1)
                if on[1]:
                    r = (j - 1) % 2
                    act.wait_ge(pT_made, pair)
                    act.wait_ge(att_made, upto(pair - 2))
                    act.copy(pT[:, r], ps_pT[0:KEYS, 0:2 * P]).then_inc(pT_copied, 1)
                if on[2]:
                    r = (j - 2) % 2
                    act.wait_ge(x2T_made, upto(pair - 1))
                    act.wait_ge(logits_made, upto(pair - 3))
                    act.copy(x2T[:, r], ps_x2T[:].rearrange("p (k t) -> p k t", k=KD)).then_inc(x2T_copied, 1)

            steps_of_part1(act, step1)

            def w1_high(e, par, b):
                w1h, raw = (a[:].rearrange("p k (b h) -> p (k b) h", b=2) for a in (w1_hi[par], w1_raw))
                act.copy(w1h[:, b], raw[:, b]).then_inc(w1_hi_made, 1)

            def w2_high(e, par, b):
                w2h, raw = (a[:].rearrange("p (b c) d -> p b (c d)", b=4) for a in (w2_hi[par], w2_raw))
                act.copy(w2h[:, b], raw[:, b]).then_inc(w2_hi_made, 1)

            act.wait_ge(w1_in, 16)
            for b in range(4):
                w1_high(0, 0, b)
            act.wait_ge(w2_in, 16)
            for b in range(4):
                w2_high(0, 0, b)

            def input_high(it, u):
                unit, N = BODY * it + u, unit_cols(u)
                for k in range(KD):
                    act.wait_ge(turned, unit + 1)
                    act.wait_ge(up_made, upto(HC * (unit - 1) + 1))
                    act.copy(in_hi[u % 2][:, k, 0:N], ps_turn[k][:, 0:N]).then_inc(in_hi_made, 1)

            def gelu(it, u, c):
                unit, N = BODY * it + u, unit_cols(u)
                e, chunk = 2 * it + u // UE, HC * u + c
                n = HC * unit + c
                act.wait_ge(up_made, n + 2)
                act.wait_ge(h_lo_made, upto(n - 2))
                act.sem_inc(act_waits, 1)
                act.activation(h_f32[:, chunk % 3, 0:N], ps_up[chunk % 3][:, 0:N], ACT.Gelu, bias=cols(b1T, HC * e + c, 1)).then_inc(gelu_made, 1)

            act.wait_ge(prep_dve, 12)
            input_high(0, 0)
            for c in range(HC):
                gelu(0, 0, c)
            input_high(0, 1)

            def step3(it, u, last):
                unit = BODY * it + u
                e, par = 2 * it + u // UE, (u // UE + 1) % 2
                for c in range(HC):
                    if not last or u + 1 < BODY:
                        gelu(it, u + 1, c)
                    if c % 2 == 1 and (not last or u < UE):
                        if u % UE == 0:
                            act.wait_ge(w1_in, 16 * (e + 2))
                            act.wait_ge(up_made, HC * unit + 1)
                            w1_high(e + 1, par, c // 2)
                        if u % UE == 1:
                            act.wait_ge(w2_in, 16 * (e + 2))
                            act.wait_ge(down_made, upto(UT * (unit - 1) + 1))
                            w2_high(e + 1, par, c // 2)
                if not last or u + 2 < BODY:
                    input_high(it, u + 2)

            steps_of_part3(act, step3)

        @block.vector
        def _(dve):

            for begun in (y_summed, y_ready):
                dve.sem_inc(begun, 1)

            dve.memset(zeros[:], 0.0).then_inc(zeroed, 1)
            dve.memset(ones[:], 1.0).then_inc(zeroed, 1)
            dve.memset(before[:], -1.0).then_inc(zeroed, 1)
            dve.memset(scan_keep[:], 1.0).then_inc(zeroed, 1)
            dve.memset(ones_bf[:], 1.0).then_inc(zeroed, 1)
            dve.memset(mean_w[:], 1.0 / D).then_inc(zeroed, 1)
            dve.memset(gathered[:], 0.0).then_inc(zeroed, 1)

            done = 0

            def prep(ins):
                nonlocal done
                done += 1
                ins.then_inc(prep_dve, 1)

            dve.wait_ge(attn_in, 16 * 9)
            dve.wait_ge(zeroed, 7)
            for k in range(KD):
                prep(dve.tensor_scalar(bq_wide[:, k, :], ones[:], bq_sb[:, k:k + 1], None, ALU.mult))
            dve.wait_ge(prep_pe, 1)
            prep(dve.tensor_copy(ctxT[:, 0, :], bank[0][:, 0:B * KEYS]))
            prep(dve.tensor_copy(ctxT[0:CR, 1, :], bank[0][0:CR, B * KEYS:2 * B * KEYS]))
            dve.wait_ge(prep_pe, 2)
            prep(dve.tensor_copy(wqT[:], bank[1][:].rearrange("p (k i) -> p k i", k=KD)))
            dve.wait_ge(prep_pe, 3)
            for k in range(KD):
                prep(dve.tensor_scalar(keyT[:, k], bank[2][:, k * D:(k + 1) * D], bk_sb[:, k:k + 1], float(D) ** -0.5, ALU.add, ALU.mult))
            dve.wait_ge(prep_pe, 4)
            prep(dve.tensor_tensor(v_sb[:, 0:2], bank[3][0:KEYS].rearrange("p (b d) -> p b d", b=2), bv_sb[:].rearrange("p (o d) -> p o d", o=1).to_broadcast([KEYS, 2, D]), ALU.add))
            prep(dve.tensor_tensor(v_sb[:, 2:4], bank[4][0:KEYS].rearrange("p (b d) -> p b d", b=2), bv_sb[:].rearrange("p (o d) -> p o d", o=1).to_broadcast([KEYS, 2, D]), ALU.add))
            dve.wait_ge(prep_pe, 5)
            prep(dve.tensor_copy(a_raw[:], bank[5][:].rearrange("p (k i) -> p k i", k=KD)))
            prep(dve.tensor_copy(c_sb[:], bank[6][:, 0:B * KEYS]))
            dve.wait_ge(prep_pe, 6)
            prep(dve.tensor_copy(b1T[:], bank[0][:, 0:E * HC]))
            prep(dve.tensor_copy(wgT[:], bank[0][:, E * HC:E * HC + KD * E].rearrange("p (k e) -> p k e", k=KD)))
            dve.wait_ge(prep_pe, 7)
            dve.wait_ge(prep_dve, 10)
            prep(dve.tensor_tensor(a_sb[:], a_raw[:], bank[7][:, 0:D].rearrange("p (o i) -> p o i", o=1).to_broadcast([P, KD, D]), ALU.subtract))
            dve.wait_ge(prep_dve, 14)

            def step1(it, j, on):
                pair = 4 * it + j
                if on[3]:
                    r = (j - 3) % 2
                    logits = ps_logit[:, 0:2 * E].rearrange("p (t e) -> p t e", t=2)
                    dve.wait_ge(logits_made, upto(pair - 2))
                    dve.tensor_reduce(gmax[:, r], logits, AX.X, ALU.max).then_inc(gmax_made, 1)
                    dve.wait_ge(gmax_made, upto(pair - 2))
                    dve.tensor_tensor(gsub[:, r], logits, gmax[:, r].rearrange("p (t o) -> p t o", o=1).to_broadcast([P, 2, E]), ALU.subtract).then_inc(gsub_made, 1)
                if on[0]:
                    r, ring = j % 2, j % 4
                    dve.wait_ge(x_in[ring], 16 * (it + 1))
                    for t in range(2):
                        ins = dve.bn_stats(stat1[:, r, t], x_sb[:, ring, t])
                    ins.then_inc(stats1_made, 1)
                    dve.wait_ge(stats1_made, pair + 1)
                    dve.wait_ge(var1_made, upto(pair - 1))
                    dve.sem_inc(dve_waits, 1)
                    for t in range(2):
                        ins = dve.bn_aggr(mv1[:, r, t], stat1[:, r, t])
                    ins.then_inc(mv1_made, 1)
                if on[3]:
                    r, ring = (j - 3) % 2, (j - 3) % 4
                    dve.wait_ge(gexp_made, upto(pair - 2))
                    dve.tensor_reduce(gsum[:, r], gexp[:, r], AX.X, ALU.add).then_inc(gsum_made, 1)
                    dve.wait_ge(gsum_made, upto(pair - 2))
                    dve.reciprocal(ginv[:, r], gsum[:, r]).then_inc(ginv_made, 1)
                    dve.wait_ge(ginv_made, upto(pair - 2))
                    to = gates[:, 2 * (pair - 3):2 * (pair - 3) + 2, :] if isinstance(it, int) else gates[:, bass.ds(2 * (pair - 3), 2), :]
                    inv = ginv[:, r].rearrange("p (t o) -> p t o", o=1).to_broadcast([P, 2, E])
                    dve.tensor_tensor(to, gexp[:, r], inv, ALU.mult).then_inc(gates_made, 1)
                    dve.tensor_tensor(rows[:, ring, :, D:ROW], gexp[:, r], inv, ALU.mult).then_inc(rows_gated, 1)
                if on[0]:
                    r = j % 2
                    dve.wait_ge(scores_made, pair + 1)
                    dve.wait_ge(rstd1_made, pair + 1)
                    dve.wait_ge(probs_made, upto(pair - 1))
                    bias = cols(c_sb, KEYS * it, KEYS)
                    for t in range(2):
                        ins = dve.scalar_tensor_tensor(out=score[:, r, t], in0=ps_score[:, t * KEYS:(t + 1) * KEYS], scalar=rstd1[:, r, t:t + 1],
                                                       in1=bias, op0=ALU.mult, op1=ALU.add)
                    ins.then_inc(scores_read, 1)
                    dve.wait_ge(scores_read, pair + 1)
                    dve.tensor_reduce(nmax[:, r], score[:, r], AX.X, ALU.max, negate=True).then_inc(score_scaled, 1)
                if on[1]:
                    r, ring = (j - 1) % 2, (j - 1) % 4
                    dve.wait_ge(probs_made, pair)
                    dve.reciprocal(pinv[:, r], psum_row[:, r]).then_inc(pinv_made, 1)
                    dve.wait_ge(pinv_made, pair)
                    dve.wait_ge(att_made, pair)
                    dve.wait_ge(x1_stored[r], upto(16 * (2 * it + (j - 1) // 2)))
                    dve.wait_ge(rows_made, upto(pair - 2))
                    for t in range(2):
                        ins = dve.scalar_tensor_tensor(out=x1[:, r, t], in0=ps_att[:, t * D:(t + 1) * D], scalar=pinv[:, r, t:t + 1],
                                                       in1=x_sb[:, ring, t], op0=ALU.mult, op1=ALU.add)
                    ins.then_inc(x1_made, 1)
                    dve.wait_ge(x1_made, pair)
                    for t in range(2):
                        ins = dve.bn_stats(stat2[:, r, t], x1[:, r, t])
                    ins.then_inc(stats2_made, 1)
                    dve.wait_ge(stats2_made, pair)
                    dve.sem_inc(dve_waits, 1)
                    for t in range(2):
                        ins = dve.bn_aggr(mv2[:, r, t], stat2[:, r, t])
                    ins.then_inc(mv2_made, 1)

            steps_of_part1(dve, step1)

            n = 0

            def then(ins):
                nonlocal n
                n += 1
                ins.then_inc(route, 1)
                dve.wait_ge(route, n)

            def wide(ap):
                return ap.rearrange("p (t o) -> p t o", o=1).to_broadcast([P, TILES, E])

            dve.wait_ge(rows_gated, PAIRS)
            left = gates
            for k in range(TOP_K):
                then(dve.tensor_reduce(best[:, k], left[:], AX.X, ALU.max))
                then(dve.tensor_tensor(same[:], left[:], wide(best[:, k]), ALU.is_equal))
                then(dve.tensor_tensor(same[:], same[:], iota_e8[:], ALU.mult))
                then(dve.tensor_reduce(choice[:, k], same[:], AX.X, ALU.min))
                then(dve.tensor_tensor(hot[:, k], iota_e8[:], wide(choice[:, k]), ALU.is_equal))
                if k == 0:
                    then(dve.scalar_tensor_tensor(out=rest[:], in0=hot[:, 0], scalar=-2.0, in1=gates[:], op0=ALU.mult, op1=ALU.add))
                    left = rest
            hot_view = hot[:].rearrange("p k t e -> p k e t")
            dve.wait_ge(counts_made, 1)
            then(dve.tensor_tensor_scan(running[:].rearrange("p m t -> p (m t)"), scan_keep[:].rearrange("p m t -> p (m t)"), ps_total[:], 0.0, ALU.mult, ALU.add))
            then(dve.tensor_tensor(place[:].rearrange("p m t -> p (m t)"), running[:].rearrange("p m t -> p (m t)"), ps_prefix[:], ALU.add))
            for k in range(TOP_K):
                dve.tensor_tensor(picked[:, k * E:(k + 1) * E], place[:, k * E:(k + 1) * E], hot_view[:, k], ALU.mult)
            then(dve.tensor_copy(same[:], rest[:]))
            for k in range(TOP_K):
                ins = dve.tensor_reduce(count[:, k], picked[:, k * E:(k + 1) * E].rearrange("p e t -> p t e"), AX.X, ALU.add)
            then(ins)
            dve.tensor_scalar(over[:], count[:], float(C), 4.0 * NT, ALU.is_ge, ALU.mult)
            dve.scalar_tensor_tensor(out=slot[:, 0], in0=choice[:, 0], scalar=float(SLOTS), in1=count[:, 0], op0=ALU.mult, op1=ALU.add)
            then(dve.scalar_tensor_tensor(out=slot[:, 1], in0=choice[:, 1], scalar=float(SLOTS), in1=count[:, 1], op0=ALU.mult, op1=ALU.subtract))
            dve.tensor_scalar(slot[:, 0], slot[:, 0], float(SLOTS * E), None, ALU.add)
            then(dve.tensor_scalar(slot[:, 1], slot[:, 1], float(SLOTS * E + C - 1), None, ALU.add))
            then(dve.tensor_scalar(tile_f[:], slot[:], -(P - 1) / 2.0, 1.0 / P, ALU.add, ALU.mult))
            then(dve.tensor_scalar(tile_f[:], tile_f[:], ROUNDER, -ROUNDER, ALU.add, ALU.add))
            dve.scalar_tensor_tensor(out=slot_lo[:], in0=tile_f[:], scalar=-float(P), in1=slot[:], op0=ALU.mult, op1=ALU.add)
            then(dve.tensor_tensor(tile_of[:], tile_f[:], over[:], ALU.add))

            with dve.Fori(0, TILES // 2) as it:
                for r in range(4):
                    t, k = 2 * it + r // 2, r % 2
                    dve.wait_ge(hot_free, 4 * it + r + 1)
                    dve.tensor_scalar(slot_hot[:, r], iota_slot[:], cols(slot_lo[:, k], t, 1), None, ALU.is_equal)
                    dve.tensor_scalar(tile_hot[:, r], iota_tile[:], cols(tile_of[:, k], t, 1), cols(token1, t, 1), ALU.is_equal, ALU.mult).then_inc(hot_made, 1)

            dve.wait_ge(table_made, 1)
            then(dve.tensor_copy(table[:], ps_table[:, 0:2 * NT]))
            then(dve.scalar_tensor_tensor(out=table1[:], in0=table[:, 0:NT], scalar=0.0, in1=table[:, NT:2 * NT], op0=ALU.is_equal, op1=ALU.mult))
            then(dve.tensor_tensor(table1[:], table1[:], table[:, 0:NT], ALU.add))
            then(dve.scalar_tensor_tensor(out=table2[:], in0=table1[:], scalar=0.0, in1=trash[:], op0=ALU.is_equal, op1=ALU.mult))
            then(dve.tensor_tensor(table3[:], table1[:], table2[:], ALU.add))
            dve.tensor_scalar(slot_token[:], table3[:], -1.0, None, ALU.add).then_inc(slots_ready, 1)

            def input_low(it, u):
                unit, N, ring = BODY * it + u, unit_cols(u), u % 3
                e = 2 * it + u // UE
                for k in range(KD):
                    dve.wait_ge(in_hi_made, KD * unit + k + 1)
                    dve.tensor_tensor(in_lo[u % 2][:, k, 0:N], ps_turn[k][:, 0:N], in_hi[u % 2][:, k, 0:N].bitcast(F32), ALU.subtract).then_inc(in_lo_made, 1)
                gate = gathered[:, ring, :, D + e:D + e + 1] if isinstance(e, int) else gathered[:, ring, :, bass.ds(D + e, 1)]
                dve.wait_ge(y_ready, upto(UT * (unit - 2) + 1))
                dve.tensor_copy(gate_of[:, ring], gate.rearrange("p j o -> p (j o)")).then_inc(gate_copied, 1)

            def hidden_parts(it, u):
                unit, N = BODY * it + u, unit_cols(u)
                dve.wait_ge(down_made, upto(UT * (unit - 1) + 1))

                def low(c):
                    chunk = HC * u + c
                    dve.wait_ge(h_hi_made, HC * unit + c + 1)
                    dve.tensor_tensor(h_lo[u % 2][:, c, 0:N], h_f32[:, chunk % 3, 0:N], h_hi[u % 2][:, c, 0:N].bitcast(F32), ALU.subtract).then_inc(h_lo_made, 1)

                for c in range(HC):
                    chunk = HC * u + c
                    dve.wait_ge(gelu_made, HC * unit + c + 1)
                    dve.tensor_copy(h_hi[u % 2][:, c, 0:N], h_f32[:, chunk % 3, 0:N]).then_inc(h_hi_made, 1)
                    if c:
                        low(c - 1)
                low(HC - 1)

            input_low(0, 0)
            hidden_parts(0, 0)
            input_low(0, 1)

            def step3(it, u, last):
                unit, par = BODY * it + u, (u // UE) % 2
                if not last or u + 1 < BODY:
                    hidden_parts(it, u + 1)
                if not last or u + 2 < BODY:
                    input_low(it, u + 2)
                if u % UE == 0:
                    dve.wait_ge(b2_in[par], 16 * (it + 1))
                dve.wait_ge(y_added, 16 * (UT * unit + 1))
                for j in range(UT):
                    m, tile = tile_rows(u, j), UT * unit + j
                    dve.wait_ge(down_made, tile + 2)
                    dve.tensor_tensor(y_sum[0:m, j], ps_y[j][0:m, 0:D], b2_wide[0:m, par], ALU.add).then_inc(y_summed, 1)
                    dve.wait_ge(y_summed, tile + 2)
                    dve.tensor_scalar(y_out[0:m, j], y_sum[0:m, j], gate_of[0:m, u % 3, j:j + 1], None, ALU.mult).then_inc(y_ready, 1)

            steps_of_part3(dve, step3)

        @block.tensor
        def _(pe):

            for begun in (up_made, down_made):
                pe.sem_inc(begun, 1)
            pe.sem_inc(hot_free, 4)

            pe.wait_ge(attn_in, 16 * 9)
            pe.wait_ge(consts, 1)
            for n in range(2):
                pe.transpose(bank[0][:, n * P:(n + 1) * P], ctx_sb[:, n, 0:P], ident[:])
                ins = pe.transpose(bank[0][0:CR, B * KEYS + n * P:B * KEYS + (n + 1) * P], ctx_sb[:, n, P:CD], ident[:])
            ins.then_inc(prep_pe, 1)
            for i in range(KD):
                for h in range(KD):
                    ins = pe.transpose(bank[1][:, h * D + i * P:h * D + (i + 1) * P], wq_sb[:, i, h * P:(h + 1) * P], ident[:])
            ins.then_inc(prep_pe, 1)
            pe.wait_ge(prep_dve, 4)
            for h in range(KD):
                to = bank[2][:, h * D:h * D + B * KEYS]
                pe.matmul(to, wk_sb[:, 0, h * P:(h + 1) * P], ctxT[:, 0, :], start=True, stop=False)
                ins = pe.matmul(to, wk_sb[0:CR, 1, h * P:(h + 1) * P], ctxT[0:CR, 1, :], start=False, stop=True)
            ins.then_inc(prep_pe, 1)
            for b in range(B):
                to = bank[3 + b // 2][0:KEYS, (b % 2) * D:(b % 2 + 1) * D]
                pe.matmul(to, ctxT[:, 0, b * KEYS:(b + 1) * KEYS], wv_sb[:, 0, :], start=True, stop=False)
                ins = pe.matmul(to, ctxT[0:CR, 1, b * KEYS:(b + 1) * KEYS], wv_sb[0:CR, 1, :], start=False, stop=True)
            ins.then_inc(prep_pe, 1)
            pe.wait_ge(prep_dve, 7)
            for i in range(KD):
                for h in range(KD):
                    pe.matmul(bank[5][:, i * D:(i + 1) * D], wqT[:, h, i * P:(i + 1) * P], keyT[:, h, :], start=(h == 0), stop=(h == KD - 1))
            for h in range(KD):
                ins = pe.matmul(bank[6][:, 0:B * KEYS], bq_wide[:, h, :], keyT[:, h, :], start=(h == 0), stop=(h == KD - 1))
            ins.then_inc(prep_pe, 1)
            pe.wait_ge(b1_in, 16)
            pe.wait_ge(wg_in, 16)
            pe.transpose(bank[0][:, 0:E * HC], b1_sb[:], ident[0:E * HC, 0:E * HC])
            for k in range(KD):
                ins = pe.transpose(bank[0][:, E * HC + k * E:E * HC + (k + 1) * E], wg_sb[:, k * P:(k + 1) * P], ident[0:E, 0:E])
            ins.then_inc(prep_pe, 1)
            pe.wait_ge(prep_dve, 10)
            for k in range(KD):
                ins = pe.matmul(bank[7][:, 0:D], mean_w[:], a_raw[:, k, :], start=(k == 0), stop=(k == KD - 1))
            ins.then_inc(prep_pe, 1)
            pe.wait_ge(prep_dve, 14)

            def step1(it, j, on):
                pair = 4 * it + j
                if on[0]:
                    pe.wait_ge(x_in[j % 4], 16 * (it + 1))
                    pe.wait_ge(xT_copied, pair)
                    for k in range(KD):
                        for t in range(2):
                            at = k * 2 * P + t * P
                            ins = pe.transpose(ps_xT[:, at:at + P], x_sb[:, j % 4, t, k * P:(k + 1) * P], ident[:])
                    ins.then_inc(xT_made, 1)
                if on[1]:
                    r = (j - 1) % 2
                    pe.wait_ge(probs_made, pair)
                    pe.wait_ge(pT_copied, upto(pair - 1))
                    pe.sem_inc(pe_waits, 1)
                    for t in range(2):
                        ins = pe.transpose(ps_pT[0:KEYS, t * P:(t + 1) * P], prob[:, r, t], ident[:])
                    ins.then_inc(pT_made, 1)
                if on[0]:
                    r = j % 2
                    pe.wait_ge(xT_copied, pair + 1)
                    pe.wait_ge(scores_read, pair)
                    for t in range(2):
                        for k in range(KD):
                            ins = pe.matmul(ps_score[:, t * KEYS:(t + 1) * KEYS], xT[:, r, k, t * P:(t + 1) * P],
                                            cols(a_sb[:, k], KEYS * it, KEYS), start=(k == 0), stop=(k == KD - 1))
                    ins.then_inc(scores_made, 1)
                if on[1]:
                    r = (j - 1) % 2
                    batch = it + (j - 1) // 4
                    v = v_sb[:, batch] if isinstance(batch, int) else v_sb[:, bass.ds(batch, 1)].rearrange("p o d -> p (o d)")
                    pe.wait_ge(pT_copied, pair)
                    pe.wait_ge(x1_made, upto(pair - 1))
                    pe.sem_inc(pe_waits, 1)
                    for t in range(2):
                        ins = pe.matmul(ps_att[:, t * D:(t + 1) * D], pT[:, r, t * P:(t + 1) * P], v, start=True, stop=True)
                    ins.then_inc(att_made, 1)
                if on[2]:
                    r, ring = (j - 2) % 2, (j - 2) % 4
                    pe.wait_ge(rows_made, upto(pair - 1))
                    pe.wait_ge(x2T_copied, upto(pair - 2))
                    for k in range(KD):
                        for t in range(2):
                            at = k * 2 * P + t * P
                            ins = pe.transpose(ps_x2T[:, at:at + P], rows[:, ring, t, k * P:(k + 1) * P], ident[:])
                    ins.then_inc(x2T_made, 1)
                    pe.wait_ge(x2T_copied, upto(pair - 1))
                    pe.wait_ge(gsub_made, upto(pair - 2))
                    for t in range(2):
                        for k in range(KD):
                            ins = pe.matmul(ps_logit[:, t * E:(t + 1) * E], x2T[:, r, k, t * P:(t + 1) * P], wgT[:, k, :],
                                            start=(k == 0), stop=(k == KD - 1))
                    ins.then_inc(logits_made, 1)

            steps_of_part1(pe, step1)

            pe.wait_ge(route, 11)
            moving = hot[:].rearrange("p k t e -> p k e t")
            for k in range(TOP_K):
                half = slice(k * E * TILES, (k + 1) * E * TILES)
                pe.matmul(ps_total[:, half], ones_bf[:], moving[:, k], start=True, stop=True)
                ins = pe.matmul(ps_prefix[:, half], before[:], moving[:, k], start=True, stop=True)
            ins.then_inc(counts_made, 1)
            pe.matmul(ps_table[:, 0:2 * NT], zeros[:, 0:P], zeros[:, 0:2 * NT], start=True, stop=False, skip_group_check=True)
            with pe.Fori(0, TILES // 2) as it:
                for r in range(4):
                    k = r % 2
                    pe.wait_ge(hot_made, 4 * it + r + 1)
                    pe.matmul(ps_table[:, k * NT:(k + 1) * NT], slot_hot[:, r], tile_hot[:, r], start=False, stop=False,
                              skip_group_check=True).then_inc(hot_free, 1)
            pe.matmul(ps_table[:, 0:2 * NT], zeros[:, 0:P], zeros[:, 0:2 * NT], start=False, stop=True, skip_group_check=True).then_inc(table_made, 1)

            def turn(it, u):
                unit, ring = BODY * it + u, u % 3
                pe.wait_ge(rows_in[ring], 16 * UT * (2 * it + u // 3 + 1))
                pe.wait_ge(in_lo_made, KD * unit)
                for k in range(KD):
                    for j in range(UT):
                        m = tile_rows(u, j)
                        ins = pe.transpose(ps_turn[k][:, j * P:j * P + m], gathered[0:m, ring, j, k * P:(k + 1) * P], ident[0:m, 0:m])
                ins.then_inc(turned, 1)

            def up(it, u):
                unit, N, e, par = BODY * it + u, unit_cols(u), 2 * it + u // UE, (u // UE) % 2
                pe.wait_ge(in_hi_made, KD * (unit + 1))
                pe.wait_ge(in_lo_made, KD * (unit + 1))
                if u % UE == 0:
                    pe.wait_ge(w1_hi_made, 4 * e + 4)
                    pe.wait_ge(w1_lo_made, 4 * e + 4)
                for c in range(HC):
                    chunk, cut = HC * u + c, slice(c * P, (c + 1) * P)
                    to = ps_up[chunk % 3][:, 0:N]
                    pe.wait_ge(gelu_made, upto(HC * unit + c - 2))
                    for k in range(KD):
                        hi, lo = in_hi[u % 2][:, k, 0:N], in_lo[u % 2][:, k, 0:N]
                        pe.matmul(to, w1_hi[par][:, k, cut], hi, start=(k == 0), stop=False)
                        pe.matmul(to, w1_hi[par][:, k, cut], lo, start=False, stop=False)
                        ins = pe.matmul(to, w1_lo[par][:, k, cut], hi, start=False, stop=(k == KD - 1))
                    ins.then_inc(up_made, 1)

            def down(it, u):
                unit, e, par = BODY * it + u, 2 * it + u // UE, (u // UE) % 2
                pe.wait_ge(y_summed, UT * unit + 1)
                if u % UE == 0:
                    pe.wait_ge(w2_hi_made, 4 * e + 4)
                    pe.wait_ge(w2_lo_made, 4 * e + 4)
                for j in range(UT):
                    m = tile_rows(u, j)
                    to = ps_y[j][0:m, 0:D]
                    for c in range(HC):
                        if j == 0:
                            pe.wait_ge(h_lo_made, HC * unit + c + 1)
                        hi, lo = (h[u % 2][:, c, j * P:j * P + m] for h in (h_hi, h_lo))
                        pe.matmul(to, hi, w2_hi[par][:, c, :], start=(c == 0), stop=False)
                        pe.matmul(to, hi, w2_lo[par][:, c, :], start=False, stop=False)
                        ins = pe.matmul(to, lo, w2_hi[par][:, c, :], start=False, stop=(c == HC - 1))
                    ins.then_inc(down_made, 1)

            turn(0, 0)
            up(0, 0)
            turn(0, 1)

            def step3(it, u, last):
                if not last or u + 1 < BODY:
                    up(it, u + 1)
                if not last or u + 2 < BODY:
                    turn(it, u + 2)
                down(it, u)

            steps_of_part3(pe, step3)


_INS = ["x", "ctx_768", "L0_xattn_Wq", "L0_xattn_bq", "L0_xattn_Wk", "L0_xattn_bk", "L0_xattn_Wv", "L0_xattn_bv",
        "L0_ffn_Wg", "L0_ffn_W1", "L0_ffn_b1", "L0_ffn_W2", "L0_ffn_b2"]


def kernel(**inputs):
    import numpy as _np
    import concourse.bacc as _bacc
    from concourse import mybir as _mybir
    from concourse.bass_utils import run_bass_kernel_spmd as _run

    nc = _bacc.Bacc("TRN2", target_bir_lowering=False, num_devices=1)
    arrays, args = {}, []
    for name in _INS:
        a = _np.ascontiguousarray(inputs[name])
        arrays[f"in_{name}_dram"] = a
        args.append(nc.dram_tensor(f"in_{name}_dram", a.shape, _mybir.dt.from_np(a.dtype), kind="ExternalInput").ap())
    B, S, D = inputs["x"].shape
    args.append(nc.dram_tensor("out_0_dram", (B * S + P, D), _mybir.dt.float32, kind="ExternalOutput").ap())
    xattn_moe(nc, *args)
    r = _run(nc, [arrays], core_ids=[0])
    return r.results[0]["out_0_dram"][:B * S].reshape(B, S, D)
```

```python
from contextlib import ExitStack

import concourse.bass as bass
from concourse import mybir

P = 128
F32 = mybir.dt.float32
F32R = mybir.dt.float32r
BF16 = mybir.dt.bfloat16
I32 = mybir.dt.int32
ALU = mybir.AluOpType
ACT = mybir.ActivationFunctionType
AX = mybir.AxisListType
EPS = 1e-5
ROUNDER = 12582912.0
TOP_K = 2
CAP_RATIO = 1.05


def upto(value):
    return max(value, 0) if isinstance(value, int) else value


def xattn_moe(nc, x, ctx_in, Wq, bq, Wk, bk, Wv, bv, Wg, W1, b1, W2, b2, out):
    B, S, D = x.shape
    T = B * S
    KEYS, CD = ctx_in.shape[1:]
    E, _, H = W1.shape
    C = int(round(TOP_K * T * CAP_RATIO / E))
    TILES = T // P
    PAIRS = TILES // 2
    PB = PAIRS // B
    KD = D // P
    HC = H // P
    CR = CD - P
    ST = -(-C // P)
    UT = 3
    UE = ST // UT
    LAST = (C - (ST - 1) * P + 1) // 2 * 2
    SLOTS = ST * P
    UNITS = E * UE
    BODY = 2 * UE
    ROW = D + E
    NT = E * ST
    KG = KEYS + E
    CH = 8
    assert KD == 2 and PB == 4 and ST % UT == 0 and UE == 3 and KEYS == 64 and P < CD <= 2 * P and TILES % 2 == 0

    with ExitStack() as stack:
        def sb(name, shape, dt=F32):
            return stack.enter_context(nc.sbuf_tensor(name, shape, dt))

        def sem(name):
            return stack.enter_context(nc.semaphore(name))

        rows_dram = nc.dram_tensor("rows_scratch", (T + P, ROW), F32).ap()

        bank = [stack.enter_context(nc.psum_tensor(f"bank{i}", [P, 512], F32)) for i in range(8)]
        ps_xT, ps_score, ps_pT, ps_att = bank[0], bank[1], bank[2], bank[3:5]
        ps_prefix, ps_total, ps_table = bank[5], bank[6], bank[7]
        ps_up, ps_turn, ps_y = bank[0:3], bank[3:5], bank[5:8]

        ident = sb("ident", [P, P])
        zeros = sb("zeros", [P, ROW])
        b1_sb = sb("b1_sb", [E * HC, P])
        b1T = sb("b1T", [P, E * HC])
        slot_token = sb("slot_token", [P, NT], I32)
        unit_token = sb("unit_token", [P, BODY, UT], I32)
        w1_raw = sb("w1_raw", [P, KD, H])
        w2_raw = sb("w2_raw", [P, HC, D])
        w1_hi = [sb(f"w1_hi{i}", [P, KD, H], F32R) for i in range(2)]
        w1_lo = [sb(f"w1_lo{i}", [P, KD, H], F32R) for i in range(2)]
        w2_hi = [sb(f"w2_hi{i}", [P, HC, D], F32R) for i in range(2)]
        w2_lo = [sb(f"w2_lo{i}", [P, HC, D], F32R) for i in range(2)]
        b2_wide = sb("b2_wide", [P, 2, D])
        gathered = sb("gathered", [P, 3, UT, ROW])

        early = ExitStack()

        def tmp(name, shape, dt=F32):
            return early.enter_context(nc.sbuf_tensor(name, shape, dt))

        iota_slot = tmp("iota_slot", [P, P, CH], BF16)
        iota_tile = tmp("iota_tile", [P, NT, CH], BF16)
        tile_no = tmp("tile_no", [P, TILES], BF16)
        iota_e8 = tmp("iota_e8", [P, TILES, E])
        row1 = tmp("row1", [P, 1])
        trash = tmp("trash", [P, NT])
        before = tmp("before", [P, P], BF16)
        ones_bf = tmp("ones_bf", [P, P], BF16)
        ones = tmp("ones", [P, P])
        zeros_bf = tmp("zeros_bf", [P, 4 * NT], BF16)
        mean_w = tmp("mean_w", [P, P])
        minus_half = tmp("minus_half", [P, 2])
        scan_keep = tmp("scan_keep", [P, TOP_K * E, TILES])
        wq_sb = tmp("wq_sb", [P, KD, D])
        wk_sb = tmp("wk_sb", [P, 2, D])
        wv_sb = tmp("wv_sb", [P, 2, ROW])
        ctx_sb = tmp("ctx_sb", [P, 2, CD])
        ctxT = tmp("ctxT", [P, 2, B * KEYS])
        ctxT_twice = tmp("ctxT_twice", [P, 2, B, 2, KEYS])
        bq_sb = tmp("bq_sb", [P, KD])
        bk_sb = tmp("bk_sb", [P, KD])
        bq_wide = tmp("bq_wide", [P, KD, P])
        bv_col = tmp("bv_col", [P, KD])
        bv_wide = tmp("bv_wide", [P, KD, P])
        bv_sb = tmp("bv_sb", [P, ROW])
        wqT = tmp("wqT", [P, KD, D])
        wvT = tmp("wvT", [P, KD, CD])
        keyT = tmp("keyT", [P, KD, B * KEYS])
        a_raw = tmp("a_raw", [P, KD, B * KEYS])
        a_sb = tmp("a_sb", [P, KD, B, KG])
        c_sb = tmp("c_sb", [P, B * KEYS])
        v_sb = tmp("v_sb", [P, B, ROW])
        v_first = tmp("v_first", [P, ROW])
        v_rest = tmp("v_rest", [P, ROW])
        wg_sb = tmp("wg_sb", [E, D])
        wg_mean = tmp("wg_mean", [E, 2])
        wg_mid = tmp("wg_mid", [E, D])
        wgT = tmp("wgT", [P, KD, E])
        x_sb = tmp("x_sb", [P, 4, 2, ROW])
        xT = tmp("xT", [P, 2, KD, 2 * P])
        stat1 = tmp("stat1", [P, 2, 2, 6])
        mv1 = tmp("mv1", [P, 2, 2, 2])
        var1 = tmp("var1", [P, 2, 2])
        rstd1 = tmp("rstd1", [P, 2, 2])
        score = tmp("score", [P, 2, 2, KEYS])
        nmax = tmp("nmax", [P, 2, 2])
        prob = tmp("prob", [P, 2, 2, KEYS])
        psum_row = tmp("psum_row", [P, 2, 2])
        pinv = tmp("pinv", [P, 2, 2])
        pT = tmp("pT", [P, 2, P])
        x1 = tmp("x1", [P, 2, 2, ROW])
        stat2 = tmp("stat2", [P, 2, 2, 6])
        mv2 = tmp("mv2", [P, 2, 2, 2])
        var2 = tmp("var2", [P, 2, 2])
        nmean2 = tmp("nmean2", [P, 2, 2])
        rstd2 = tmp("rstd2", [P, 2, 2])
        shift2 = tmp("shift2", [P, 2, 2])
        rows = tmp("rows", [P, 4, 2, ROW])
        gmax = tmp("gmax", [P, 2, 4])
        gsub = tmp("gsub", [P, 2, 4, E])
        gexp = tmp("gexp", [P, 2, 4, E])
        gsum = tmp("gsum", [P, 2, 4])
        ginv = tmp("ginv", [P, 2, 4])
        gates = tmp("gates", [P, TILES, E])
        best = tmp("best", [P, TOP_K, TILES])
        same = tmp("same", [P, TILES, E])
        choice = tmp("choice", [P, TOP_K, TILES])
        hot = tmp("hot", [P, TOP_K, TILES, E], BF16)
        rest = tmp("rest", [P, TILES, E])
        running = tmp("running", [P, TOP_K * E, TILES])
        place = tmp("place", [P, TOP_K * E, TILES])
        picked = tmp("picked", [P, TOP_K * E, TILES])
        count = tmp("count", [P, TOP_K, TILES])
        over = tmp("over", [P, TOP_K, TILES])
        slot = tmp("slot", [P, TOP_K, TILES])
        tile_f = tmp("tile_f", [P, TOP_K, TILES])
        slot_lo = tmp("slot_lo", [P, TOP_K, TILES], BF16)
        tile_of = tmp("tile_of", [P, TOP_K, TILES], BF16)
        slot_hot = tmp("slot_hot", [P, TOP_K, P, CH], BF16)
        tile_hot = tmp("tile_hot", [P, TOP_K, NT, CH], BF16)
        tokens_hot = tmp("tokens_hot", [P, TOP_K, 2, NT, CH], BF16)
        table = tmp("table", [P, TOP_K, 2, NT])
        table0 = tmp("table0", [P, TOP_K, NT])
        table1 = tmp("table1", [P, NT])
        table2 = tmp("table2", [P, NT])
        early.close()

        gate_of = sb("gate_of", [P, 3, UT])
        in_hi = [sb(f"in_hi{i}", [P, KD, UT * P], F32R) for i in range(2)]
        in_lo = [sb(f"in_lo{i}", [P, KD, UT * P], F32R) for i in range(2)]
        h_f32 = sb("h_f32", [P, 3, UT * P])
        h_hi = [sb(f"h_hi{i}", [P, HC, UT * P], F32R) for i in range(2)]
        h_lo = [sb(f"h_lo{i}", [P, HC, UT * P], F32R) for i in range(2)]
        y_sum = sb("y_sum", [P, UT, D])
        y_out = sb("y_out", [P, UT, D])

        attn_in, b1_in, wg_in = sem("attn_in"), sem("b1_in"), sem("wg_in")
        consts = sem("consts")
        zeroed = sem("zeroed")
        prep_pe, prep_dve, prep_act = sem("prep_pe"), sem("prep_dve"), sem("prep_act")

        pool_waits, act_waits, dve_waits, pe_waits = sem("pool_waits"), sem("act_waits"), sem("dve_waits"), sem("pe_waits")

        x_in = [sem(f"x_in{i}") for i in range(4)]
        xT_made, xT_copied, scores_made, scores_read = sem("xT_made"), sem("xT_copied"), sem("scores_made"), sem("scores_read")
        xg_copied, v_first_made, v_rest_made = sem("xg_copied"), sem("v_first_made"), sem("v_rest_made")
        stats1_made, mv1_made, var1_made, rstd1_made = sem("stats1_made"), sem("mv1_made"), sem("var1_made"), sem("rstd1_made")
        score_scaled = sem("score_scaled")
        probs_made, pT_made, pT_copied, att_made = sem("probs_made"), sem("pT_made"), sem("pT_copied"), sem("att_made")
        pinv_made, x1_made, stats2_made, mv2_made = sem("pinv_made"), sem("x1_made"), sem("stats2_made"), sem("mv2_made")
        var2_made, rstd2_made, shift2_made, rows_made = sem("var2_made"), sem("rstd2_made"), sem("shift2_made"), sem("rows_made")
        x1_stored = [sem(f"x1_stored{i}") for i in range(2)]
        rows_stored = [sem(f"rows_stored{i}") for i in range(2)]
        gmax_made, gsub_made, gexp_made, gsum_made, ginv_made, gates_made, rows_gated = (
            sem("gmax_made"), sem("gsub_made"), sem("gexp_made"), sem("gsum_made"), sem("ginv_made"),
            sem("gates_made"), sem("rows_gated"))

        route = sem("route")
        counts_made = sem("counts_made")
        tile_hot_made, hot_made, hot_free = sem("tile_hot_made"), sem("hot_made"), sem("hot_free")
        table_made, slots_ready = sem("table_made"), sem("slots_ready")

        w1_in, w2_in = sem("w1_in"), sem("w2_in")
        b2_in = [sem("b2_in0"), sem("b2_in1")]
        w1_hi_made, w1_lo_made, w2_hi_made, w2_lo_made = sem("w1_hi_made"), sem("w1_lo_made"), sem("w2_hi_made"), sem("w2_lo_made")
        rows_in = [sem(f"rows_in{i}") for i in range(3)]
        unit_token_made, gate_copied = sem("unit_token_made"), sem("gate_copied")
        turned, in_hi_made, in_lo_made = sem("turned"), sem("in_hi_made"), sem("in_lo_made")
        up_made, gelu_made, h_hi_made, h_lo_made = sem("up_made"), sem("gelu_made"), sem("h_hi_made"), sem("h_lo_made")
        down_made, y_summed, y_ready, y_added = sem("down_made"), sem("y_summed"), sem("y_ready"), sem("y_added")

        x_pairs = x.rearrange("b s d -> (b s) d").rearrange("(n t p) d -> n p t d", t=2, p=P)
        out_pairs = out[0:T, :].rearrange("(n t p) d -> n p t d", t=2, p=P)
        rows_batches = rows_dram[0:T, :].rearrange("(n t p) d -> n p t d", t=4, p=P)
        w1_view = W1.rearrange("e (k p) h -> e p k h", p=P)
        w2_view = W2.rearrange("e (c p) d -> e p c d", p=P)

        def one(view, i):
            if isinstance(i, int):
                return view[i]
            names = "abc"[:len(view.shape) - 1]
            return view[bass.ds(i, 1)].rearrange(f"o {' '.join(names)} -> (o {names[0]}) {' '.join(names[1:])}")

        def cols(ap, start, size):
            return ap[:, start:start + size] if isinstance(start, int) else ap[:, bass.ds(start, size)]

        def steps_of_part1(eng, step):
            for s in range(PB):
                step(0, s, [s - lag >= 0 for lag in range(5)])
            with eng.Fori(1, PAIRS // PB) as it:
                for j in range(PB):
                    step(it, j, [True] * 5)
            for s in range(PAIRS, PAIRS + PB):
                step(PAIRS // PB, s - PAIRS, [s - lag < PAIRS for lag in range(5)])

        def gates_due(it, j):
            return j % 2 == 1 and not (isinstance(it, int) and it == 0)

        def gate_batch(it, j):
            return 2 * it + (j - 3) // 2

        def steps_of_part3(eng, step):
            with eng.Fori(0, UNITS // BODY - 1) as it:
                for u in range(BODY):
                    step(it, u, False)
            for u in range(BODY):
                step(UNITS // BODY - 1, u, True)

        def tile_rows(u, j):
            return LAST if u % UE == UE - 1 and j == UT - 1 else P

        def unit_cols(u):
            return (UT - 1) * P + tile_rows(u, UT - 1)

        block = stack.enter_context(nc.Block())

        @block.sync
        def _(sp):
            def load_x(pair, ring):
                sp.dma_start(x_sb[:, ring, :, 0:D], one(x_pairs, pair)).then_inc(x_in[ring], 16)

            sp.dma_start(ctx_sb[:], ctx_in.rearrange("b k c -> (b k) c").rearrange("(n p) c -> p n c", p=P)).then_inc(attn_in, 16)
            for w, t in ((Wk, wk_sb), (Wv, wv_sb)):
                sp.dma_start(t[:, 0, 0:D], w[0:P, :]).then_inc(attn_in, 16)
                sp.dma_start(t[0:CR, 1, 0:D], w[P:CD, :]).then_inc(attn_in, 16)
            sp.dma_start(wq_sb[:], Wq.rearrange("(k p) h -> p k h", p=P)).then_inc(attn_in, 16)
            with nc.allow_non_contiguous_dma(reason="two columns of 128 biases"):
                sp.dma_start(bq_sb[:], bq.rearrange("(k p) -> p k", p=P)).then_inc(attn_in, 16)
                sp.dma_start(bk_sb[:], bk.rearrange("(k p) -> p k", p=P)).then_inc(attn_in, 16)
                sp.dma_start(bv_col[:], bv.rearrange("(k p) -> p k", p=P)).then_inc(attn_in, 16)
            sp.dma_start(bv_sb[:, 0:D], bv.rearrange("(o d) -> o d", o=1).to_broadcast([P, D])).then_inc(attn_in, 16)
            sp.dma_start(wg_sb[:], Wg).then_inc(wg_in, 16)
            load_x(0, 0)
            sp.dma_start(b1_sb[:], b1.rearrange("e (c p) -> (e c) p", p=P)).then_inc(b1_in, 16)
            sp.wait_ge(zeroed, 1)
            quarter = P // 4
            for i, stored in enumerate(x1_stored + rows_stored):
                sp.dma_start(rows_dram[T + i * quarter:T + (i + 1) * quarter, :], zeros[0:quarter, :]).then_inc(stored, 16)

            def load_w1(e):
                sp.dma_start(w1_raw[:], one(w1_view, e)).then_inc(w1_in, 16)

            def load_w2(e):
                sp.dma_start(w2_raw[:], one(w2_view, e)).then_inc(w2_in, 16)

            def load_b2(e, ring):
                sp.dma_start(b2_wide[:, ring], (b2[e:e + 1] if isinstance(e, int) else b2[bass.ds(e, 1)]).to_broadcast([P, D])).then_inc(b2_in[ring], 16)

            def step1(it, j, on):
                pair = 4 * it + j
                if on[0] and not (isinstance(it, int) and pair == 0):
                    sp.wait_ge(x1_made, upto(pair - 3))
                    load_x(pair, j)
                if on[4]:
                    sp.wait_ge(x1_made, pair - 3)
                    sp.dma_start(one(out_pairs, pair - 4), x1[:, j % 2, :, 0:D]).then_inc(x1_stored[j % 2], 16)

            steps_of_part1(sp, step1)

            load_w1(0)
            load_w2(0)
            load_b2(0, 0)

            def step3(it, u, last):
                e = 2 * it + u // UE
                if last and u >= UE:
                    return
                if u % UE == 0:
                    sp.wait_ge(w1_hi_made, 4 * e + 4)
                    sp.wait_ge(w1_lo_made, 4 * e + 4)
                    load_w1(e + 1)
                    sp.wait_ge(w2_hi_made, 4 * e + 4)
                    sp.wait_ge(w2_lo_made, 4 * e + 4)
                    load_w2(e + 1)
                    sp.wait_ge(y_summed, UT * UE * e + 1)
                    load_b2(e + 1, (u // UE + 1) % 2)

            steps_of_part3(sp, step3)
            sp.wait_ge(y_added, 16 * (UT * UNITS + 1))

        @block.gpsimd
        def _(pool):

            n = 0

            def const(ins):
                nonlocal n
                n += 1
                ins.then_inc(consts, 1)

            small = dict(allow_small_or_imprecise_dtypes=True)
            pool.sem_inc(rows_made, 1)
            pool.wait_ge(zeroed, 2)
            pool.dma_start(out[T:T + P, :], zeros[:, 0:D]).then_inc(y_added, 16)
            const(pool.affine_select(out=ident[:], in_=ones[:], compare_op=ALU.is_equal, fill=0.0, base=0, pattern=[[-1, P]], channel_multiplier=1))
            const(pool.memset(minus_half[:], -0.5))
            const(pool.iota(iota_slot[:], [[1, P], [0, CH]], base=0, channel_multiplier=0, **small))
            const(pool.iota(iota_tile[:], [[1, NT], [0, CH]], base=0, channel_multiplier=0, **small))
            const(pool.iota(tile_no[:], [[1, TILES]], base=0, channel_multiplier=0, **small))
            const(pool.iota(iota_e8[:], [[0, TILES], [1, E]], base=-E, channel_multiplier=0, **small))
            const(pool.iota(row1[:], [[0, 1]], base=1, channel_multiplier=1, **small))
            const(pool.iota(trash[:], [[0, NT]], base=T + 1, channel_multiplier=1, **small))
            pool.wait_ge(zeroed, 3)
            const(pool.affine_select(out=before[:], in_=before[:], compare_op=ALU.is_ge, fill=0.0, base=0, pattern=[[-1, P]], channel_multiplier=1))
            pool.wait_ge(zeroed, 4)
            const(pool.affine_select(out=scan_keep[:], in_=scan_keep[:], compare_op=ALU.is_gt, fill=0.0, base=0, pattern=[[0, TOP_K * E], [1, TILES]], channel_multiplier=0))
            pool.wait_ge(consts, n)

            def step1(it, j, on):
                pair = 4 * it + j
                if on[3]:
                    r, ring = (j - 3) % 2, (j - 3) % 4
                    pool.wait_ge(mv2_made, pair - 2)
                    pool.sem_inc(pool_waits, 1)
                    pool.tensor_scalar(var2[:, r], mv2[:, r, :, 1], 1.0, EPS, ALU.mult, ALU.add)
                    pool.tensor_scalar(nmean2[:, r], mv2[:, r, :, 0], -1.0, 0.0, ALU.mult, ALU.add).then_inc(var2_made, 1)
                    pool.wait_ge(var2_made, pair - 2)
                    pool.tensor_tensor(rstd2[:, r], var2[:, r], minus_half[:], ALU.pow).then_inc(rstd2_made, 1)
                    pool.wait_ge(rstd2_made, pair - 2)
                    pool.tensor_tensor(shift2[:, r], nmean2[:, r], rstd2[:, r], ALU.mult).then_inc(shift2_made, 1)
                    pool.wait_ge(shift2_made, pair - 2)
                    pool.wait_ge(rows_stored[ring // 2], 16 * (it + (j - 3) // 4 + 1))
                    pool.sem_inc(pool_waits, 1)
                    for t in range(2):
                        ins = pool.tensor_scalar(rows[:, ring, t], x1[:, r, t], rstd2[:, r, t:t + 1], shift2[:, r, t:t + 1], ALU.mult, ALU.add)
                    ins.then_inc(rows_made, 1)
                if on[0]:
                    r = j % 2
                    pool.wait_ge(mv1_made, pair + 1)
                    pool.wait_ge(score_scaled, upto(pair - 1))
                    pool.sem_inc(pool_waits, 1)
                    pool.tensor_scalar(var1[:, r], mv1[:, r, :, 1], 1.0, EPS, ALU.mult, ALU.add).then_inc(var1_made, 1)
                    pool.wait_ge(var1_made, pair + 1)
                    pool.tensor_tensor(rstd1[:, r], var1[:, r], minus_half[:], ALU.pow).then_inc(rstd1_made, 1)

            steps_of_part1(pool, step1)

            def w1_low(e, par):
                w1h, w1l, raw = (a[:].rearrange("p k (b h) -> p (k b) h", b=2) for a in (w1_hi[par], w1_lo[par], w1_raw))
                for b in range(4):
                    pool.wait_ge(w1_hi_made, 4 * e + b + 1)
                    pool.tensor_tensor(w1l[:, b], raw[:, b], w1h[:, b].bitcast(F32), ALU.subtract).then_inc(w1_lo_made, 1)

            def w2_low(e, par):
                w2h, w2l, raw = (a[:].rearrange("p (b c) d -> p b (c d)", b=4) for a in (w2_hi[par], w2_lo[par], w2_raw))
                for b in range(4):
                    pool.wait_ge(w2_hi_made, 4 * e + b + 1)
                    pool.tensor_tensor(w2l[:, b], raw[:, b], w2h[:, b].bitcast(F32), ALU.subtract).then_inc(w2_lo_made, 1)

            pool.wait_ge(w1_in, 16)
            w1_low(0, 0)
            pool.wait_ge(w2_in, 16)
            w2_low(0, 0)

            def gather(it, u):
                ring, index = u % 3, u % BODY
                unit = BODY * it + u
                pool.tensor_copy(unit_token[:, index], cols(slot_token, UT * unit, UT)).then_inc(unit_token_made, 1)
                pool.wait_ge(unit_token_made, unit + 1)
                pool.sem_inc(pool_waits, 1)
                for j in range(UT):
                    n_rows = tile_rows(u, j)
                    pool.indirect_dma_start(
                        gathered[0:n_rows, ring, j, :], None, rows_dram[:, :],
                        bass.IndirectOffsetOnAxis(ap=unit_token[0:n_rows, index, j:j + 1], axis=0),
                    ).then_inc(rows_in[ring], 16)

            for ring in range(2):
                pool.wait_ge(rows_stored[ring], 16 * (PAIRS // 4 + 1))
            for ring in range(2):
                pool.wait_ge(x1_stored[ring], 16 * (PAIRS // 2 + 1))
            pool.wait_ge(slots_ready, 1)
            for u in range(3):
                gather(0, u)

            def step3(it, u, last):
                unit = BODY * it + u
                e = 2 * it + u // UE
                par = (u // UE + 1) % 2
                if not last or u + 3 < BODY:
                    pool.wait_ge(turned, unit + 1)
                    pool.wait_ge(gate_copied, unit + 1)
                    gather(it, u + 3)
                if not last or u < UE:
                    if u % UE == 0:
                        w1_low(e + 1, par)
                    if u % UE == 1:
                        w2_low(e + 1, par)
                for j in range(UT):
                    n_rows, tile = tile_rows(u, j), UT * unit + j
                    pool.wait_ge(y_ready, tile + 2)
                    pool.wait_ge(y_added, 16 * (tile + 1))
                    pool.sem_inc(pool_waits, 1)
                    pool.indirect_dma_start(
                        out[:, :], bass.IndirectOffsetOnAxis(ap=unit_token[0:n_rows, u, j:j + 1], axis=0),
                        y_out[0:n_rows, j, :], None, compute_op=ALU.add,
                    ).then_inc(y_added, 16)

            steps_of_part3(pool, step3)

        @block.scalar
        def _(act):

            act.wait_ge(prep_dve, 6)
            for n, part in ((0, P), (1, CR)):
                act.copy(ctxT_twice[0:part, n], ctxT[0:part, n, :].rearrange("p (b o k) -> p b o k", b=B, o=1).to_broadcast([part, B, 2, KEYS])).then_inc(prep_act, 1)

            def step1(it, j, on):
                pair = 4 * it + j
                if on[2]:
                    r = j % 2
                    act.wait_ge(pT_made, upto(pair - 1))
                    act.wait_ge(att_made, upto(pair - 3))
                    act.copy(pT[:, r], ps_pT[:, 0:P]).then_inc(pT_copied, 1)
                if on[0]:
                    r = j % 2
                    act.wait_ge(xT_made, pair + 1)
                    act.wait_ge(scores_made, upto(pair - 1))
                    act.copy(xT[:, r], ps_xT[:].rearrange("p (k t) -> p k t", k=KD)).then_inc(xT_copied, 1)
                if on[1]:
                    act.wait_ge(scores_read, pair)
                    act.copy(x_sb[:, (j - 1) % 4, :, D:ROW], ps_score[:, 0:2 * KG].rearrange("p (t c) -> p t c", t=2)[:, :, KEYS:KG]).then_inc(xg_copied, 1)
                if on[1]:
                    r = (j - 1) % 2
                    act.wait_ge(score_scaled, pair)
                    act.wait_ge(pT_made, upto(pair - 2))
                    act.wait_ge(pinv_made, upto(pair - 2))
                    for t in range(2):
                        ins = act.activation(prob[:, r, t], score[:, r, t], ACT.Exp, bias=nmax[:, r, t:t + 1], accum_out=psum_row[:, r, t:t + 1])
                    ins.then_inc(probs_made, 1)
                if gates_due(it, j):
                    act.wait_ge(gsub_made, gate_batch(it, j))
                    act.activation(gexp[:, j // 2], gsub[:, j // 2], ACT.Exp).then_inc(gexp_made, 1)
                if on[1] and j in (1, 2):
                    v_to, v_made = (v_first, v_first_made) if j == 1 else (v_rest, v_rest_made)
                    v_now = v_sb[:, it] if isinstance(it, int) else v_sb[:, bass.ds(it, 1)].rearrange("p o d -> p (o d)")
                    act.wait_ge(prep_dve, 27)
                    act.wait_ge(att_made, upto(pair - 2))
                    act.sem_inc(act_waits, 1)
                    act.copy(v_to[:], v_now).then_inc(v_made, 1)
                if gates_due(it, j):
                    act.wait_ge(rows_gated, gate_batch(it, j))
                    act.dma_start(one(rows_batches, gate_batch(it, j) - 1), rows[:, j - 1:j + 1].rearrange("p n t d -> p (n t) d")).then_inc(rows_stored[j // 2], 16)

            steps_of_part1(act, step1)

            def w1_high(e, par, b):
                w1h, raw = (a[:].rearrange("p k (b h) -> p (k b) h", b=2) for a in (w1_hi[par], w1_raw))
                act.copy(w1h[:, b], raw[:, b]).then_inc(w1_hi_made, 1)

            def w2_high(e, par, b):
                w2h, raw = (a[:].rearrange("p (b c) d -> p b (c d)", b=4) for a in (w2_hi[par], w2_raw))
                act.copy(w2h[:, b], raw[:, b]).then_inc(w2_hi_made, 1)

            act.wait_ge(w1_in, 16)
            for b in range(4):
                w1_high(0, 0, b)
            act.wait_ge(w2_in, 16)
            for b in range(4):
                w2_high(0, 0, b)

            def input_high(it, u):
                unit, N = BODY * it + u, unit_cols(u)
                for k in range(KD):
                    act.wait_ge(turned, unit + 1)
                    act.wait_ge(up_made, upto(HC * (unit - 1) + 1))
                    act.copy(in_hi[u % 2][:, k, 0:N], ps_turn[k][:, 0:N]).then_inc(in_hi_made, 1)

            def gelu(it, u, c):
                unit, N = BODY * it + u, unit_cols(u)
                e, chunk = 2 * it + u // UE, HC * u + c
                n = HC * unit + c
                act.wait_ge(up_made, n + 2)
                act.wait_ge(h_lo_made, upto(n - 2))
                act.sem_inc(act_waits, 1)
                act.activation(h_f32[:, chunk % 3, 0:N], ps_up[chunk % 3][:, 0:N], ACT.Gelu, bias=cols(b1T, HC * e + c, 1)).then_inc(gelu_made, 1)

            act.wait_ge(prep_dve, 16)
            input_high(0, 0)
            for c in range(HC):
                gelu(0, 0, c)
            input_high(0, 1)

            def step3(it, u, last):
                unit = BODY * it + u
                e, par = 2 * it + u // UE, (u // UE + 1) % 2
                for c in range(HC):
                    if not last or u + 1 < BODY:
                        gelu(it, u + 1, c)
                    if c % 2 == 1 and (not last or u < UE):
                        if u % UE == 0:
                            act.wait_ge(w1_in, 16 * (e + 2))
                            act.wait_ge(up_made, HC * unit + 1)
                            w1_high(e + 1, par, c // 2)
                        if u % UE == 1:
                            act.wait_ge(w2_in, 16 * (e + 2))
                            act.wait_ge(down_made, upto(UT * (unit - 1) + 1))
                            w2_high(e + 1, par, c // 2)
                if not last or u + 2 < BODY:
                    input_high(it, u + 2)

            steps_of_part3(act, step3)

        @block.vector
        def _(dve):

            for begun in (y_summed, y_ready):
                dve.sem_inc(begun, 1)

            dve.memset(zeros[:], 0.0).then_inc(zeroed, 1)
            dve.memset(ones[:], 1.0).then_inc(zeroed, 1)
            dve.memset(before[:], -1.0).then_inc(zeroed, 1)
            dve.memset(scan_keep[:], 1.0).then_inc(zeroed, 1)
            dve.memset(ones_bf[:], 1.0).then_inc(zeroed, 1)
            dve.memset(mean_w[:], 1.0 / D).then_inc(zeroed, 1)
            dve.memset(zeros_bf[:], 0.0).then_inc(zeroed, 1)
            dve.memset(gathered[:], 0.0).then_inc(zeroed, 1)

            done = 0

            def prep(ins):
                nonlocal done
                done += 1
                ins.then_inc(prep_dve, 1)

            dve.wait_ge(attn_in, 16 * 10)
            dve.wait_ge(zeroed, 8)
            for k in range(KD):
                prep(dve.tensor_scalar(bq_wide[:, k, :], ones[:], bq_sb[:, k:k + 1], None, ALU.mult))
            for k in range(KD):
                prep(dve.tensor_scalar(bv_wide[:, k, :], ones[:], bv_col[:, k:k + 1], None, ALU.mult))
            dve.wait_ge(prep_pe, 1)
            prep(dve.tensor_copy(ctxT[:, 0, :], bank[0][:, 0:B * KEYS]))
            prep(dve.tensor_copy(ctxT[0:CR, 1, :], bank[0][0:CR, B * KEYS:2 * B * KEYS]))
            dve.wait_ge(prep_pe, 2)
            prep(dve.tensor_copy(wqT[:], bank[1][:].rearrange("p (k i) -> p k i", k=KD)))
            dve.wait_ge(prep_pe, 3)
            prep(dve.tensor_copy(wvT[:], bank[3][:, 0:KD * CD].rearrange("p (k i) -> p k i", k=KD)))
            dve.wait_ge(wg_in, 16)
            prep(dve.tensor_reduce(wg_mean[:, 0:1], wg_sb[:], AX.X, ALU.add))
            dve.wait_ge(prep_dve, 9)
            prep(dve.tensor_scalar(wg_mean[:, 1:2], wg_mean[:, 0:1], 1.0 / D, None, ALU.mult))
            dve.wait_ge(prep_dve, 10)
            prep(dve.tensor_scalar(wg_mid[:], wg_sb[:], wg_mean[:, 1:2], None, ALU.subtract))
            dve.wait_ge(prep_pe, 4)
            for k in range(KD):
                prep(dve.tensor_scalar(keyT[:, k], bank[2][:, k * D:(k + 1) * D], bk_sb[:, k:k + 1], float(D) ** -0.5, ALU.add, ALU.mult))
            dve.wait_ge(prep_pe, 5)
            prep(dve.tensor_copy(b1T[:], bank[0][:, 0:E * HC]))
            g_ps = bank[0][:, E * HC:E * HC + KD * E]
            prep(dve.tensor_copy(wgT[:], g_ps.rearrange("p (k e) -> p k e", k=KD)))
            prep(dve.tensor_copy(a_sb[:, :, :, KEYS:KG], g_ps.rearrange("p (k o e) -> p k o e", k=KD, o=1).to_broadcast([P, KD, B, E])))
            dve.wait_ge(prep_pe, 6)
            prep(dve.tensor_copy(a_raw[:], bank[5][:].rearrange("p (k i) -> p k i", k=KD)))
            prep(dve.tensor_copy(c_sb[:], bank[6][:, 0:B * KEYS]))
            dve.wait_ge(prep_pe, 7)
            prep(dve.tensor_copy(wv_sb[:, 0, D:ROW], bank[4][:, 0:E]))
            prep(dve.tensor_copy(wv_sb[0:CR, 1, D:ROW], bank[4][0:CR, E:2 * E]))
            prep(dve.tensor_copy(bv_sb[:, D:ROW], bank[4][:, 2 * E:3 * E]))
            dve.wait_ge(prep_pe, 8)
            dve.wait_ge(prep_dve, 17)
            for k in range(KD):
                prep(dve.tensor_tensor(a_sb[:, k, :, 0:KEYS], a_raw[:, k].rearrange("p (b i) -> p b i", b=B), bank[7][:, 0:B * KEYS].rearrange("p (b i) -> p b i", b=B), ALU.subtract))

            def values():
                dve.wait_ge(prep_pe, 9)
                dve.wait_ge(prep_dve, 21)
                for b in range(B):
                    prep(dve.tensor_tensor(v_sb[:, b], bank[(5, 6, 7, 3)[b]][:, 0:ROW], bv_sb[:], ALU.add))

            def step1(it, j, on):
                pair = 4 * it + j
                if on[3]:
                    r, ring = (j - 3) % 2, (j - 3) % 4
                    dve.wait_ge(att_made, pair - 2)
                    dve.wait_ge(xg_copied, pair - 2)
                    dve.wait_ge(pinv_made, pair - 2)
                    dve.wait_ge(x1_stored[r], 16 * (2 * it + (j - 3) // 2 + 1))
                    dve.wait_ge(rows_made, upto(pair - 3))
                    for t in range(2):
                        ins = dve.scalar_tensor_tensor(out=x1[:, r, t], in0=ps_att[t][:, 0:ROW], scalar=pinv[:, r, t:t + 1],
                                                       in1=x_sb[:, ring, t], op0=ALU.mult, op1=ALU.add)
                    ins.then_inc(x1_made, 1)
                    dve.wait_ge(x1_made, pair - 2)
                    for t in range(2):
                        ins = dve.bn_stats(stat2[:, r, t], x1[:, r, t, 0:D])
                    ins.then_inc(stats2_made, 1)
                    dve.wait_ge(stats2_made, pair - 2)
                    dve.sem_inc(dve_waits, 1)
                    for t in range(2):
                        ins = dve.bn_aggr(mv2[:, r, t], stat2[:, r, t])
                    ins.then_inc(mv2_made, 1)
                if gates_due(it, j):
                    r, batch = j // 2, gate_batch(it, j)
                    logits = rows[:, j - 1:j + 1, :, D:ROW].rearrange("p n t e -> p (n t) e")
                    dve.wait_ge(rows_made, pair - 2)
                    dve.tensor_reduce(gmax[:, r], logits, AX.X, ALU.max).then_inc(gmax_made, 1)
                    dve.wait_ge(gmax_made, batch)
                    dve.tensor_tensor(gsub[:, r], logits, gmax[:, r].rearrange("p (t o) -> p t o", o=1).to_broadcast([P, 4, E]), ALU.subtract).then_inc(gsub_made, 1)
                if on[2]:
                    r = j % 2
                    dve.wait_ge(probs_made, upto(pair - 1))
                    dve.reciprocal(pinv[:, r], psum_row[:, r]).then_inc(pinv_made, 1)
                if on[1]:
                    r, start = (j - 1) % 2, KEYS * it + KEYS * ((j - 1) // 4)
                    dve.wait_ge(scores_made, pair)
                    dve.wait_ge(rstd1_made, pair)
                    dve.wait_ge(probs_made, upto(pair - 2))
                    for t in range(2):
                        ins = dve.scalar_tensor_tensor(out=score[:, r, t], in0=ps_score[:, t * KG:t * KG + KEYS], scalar=rstd1[:, r, t:t + 1],
                                                       in1=cols(c_sb, start, KEYS), op0=ALU.mult, op1=ALU.add)
                    ins.then_inc(scores_read, 1)
                    dve.wait_ge(scores_read, pair)
                    dve.tensor_reduce(nmax[:, r], score[:, r], AX.X, ALU.max, negate=True).then_inc(score_scaled, 1)
                if on[0]:
                    r, ring = j % 2, j % 4
                    dve.wait_ge(x_in[ring], 16 * (it + 1))
                    for t in range(2):
                        ins = dve.bn_stats(stat1[:, r, t], x_sb[:, ring, t, 0:D])
                    ins.then_inc(stats1_made, 1)
                    dve.wait_ge(stats1_made, pair + 1)
                    dve.wait_ge(var1_made, upto(pair - 1))
                    dve.sem_inc(dve_waits, 1)
                    for t in range(2):
                        ins = dve.bn_aggr(mv1[:, r, t], stat1[:, r, t])
                    ins.then_inc(mv1_made, 1)
                if gates_due(it, j):
                    r, batch = j // 2, gate_batch(it, j)
                    dve.wait_ge(gexp_made, batch)
                    dve.tensor_reduce(gsum[:, r], gexp[:, r], AX.X, ALU.add).then_inc(gsum_made, 1)
                    dve.wait_ge(gsum_made, batch)
                    dve.reciprocal(ginv[:, r], gsum[:, r]).then_inc(ginv_made, 1)
                    dve.wait_ge(ginv_made, batch)
                    first = 4 * (batch - 1)
                    to = gates[:, first:first + 4, :] if isinstance(it, int) else gates[:, bass.ds(first, 4), :]
                    inv = ginv[:, r].rearrange("p (t o) -> p t o", o=1).to_broadcast([P, 4, E])
                    dve.tensor_tensor(rows[:, j - 1:j + 1, :, D:ROW].rearrange("p n t e -> p (n t) e"), gexp[:, r], inv, ALU.mult).then_inc(rows_gated, 1)
                    dve.tensor_tensor(to, gexp[:, r], inv, ALU.mult).then_inc(gates_made, 1)
                if isinstance(it, int) and it == 0 and j == 1:
                    values()

            steps_of_part1(dve, step1)

            n = 0

            def then(ins):
                nonlocal n
                n += 1
                ins.then_inc(route, 1)
                dve.wait_ge(route, n)

            def wide(ap):
                return ap.rearrange("p (t o) -> p t o", o=1).to_broadcast([P, TILES, E])

            dve.wait_ge(gates_made, PAIRS // 2)
            left = gates
            for k in range(TOP_K):
                then(dve.tensor_reduce(best[:, k], left[:], AX.X, ALU.max))
                then(dve.tensor_tensor(same[:], left[:], wide(best[:, k]), ALU.is_equal))
                then(dve.tensor_tensor(same[:], same[:], iota_e8[:], ALU.mult))
                then(dve.tensor_reduce(choice[:, k], same[:], AX.X, ALU.min))
                then(dve.tensor_tensor(hot[:, k], iota_e8[:], wide(choice[:, k]), ALU.is_equal))
                if k == 0:
                    then(dve.scalar_tensor_tensor(out=rest[:], in0=hot[:, 0], scalar=-2.0, in1=gates[:], op0=ALU.mult, op1=ALU.add))
                    left = rest
            hot_view = hot[:].rearrange("p k t e -> p k e t")
            dve.wait_ge(counts_made, 1)
            then(dve.tensor_tensor_scan(running[:].rearrange("p m t -> p (m t)"), scan_keep[:].rearrange("p m t -> p (m t)"), ps_total[:], 0.0, ALU.mult, ALU.add))
            then(dve.tensor_tensor(place[:].rearrange("p m t -> p (m t)"), running[:].rearrange("p m t -> p (m t)"), ps_prefix[:], ALU.add))
            for k in range(TOP_K):
                dve.tensor_tensor(picked[:, k * E:(k + 1) * E], place[:, k * E:(k + 1) * E], hot_view[:, k], ALU.mult)
            then(dve.tensor_copy(same[:], rest[:]))
            for k in range(TOP_K):
                ins = dve.tensor_reduce(count[:, k], picked[:, k * E:(k + 1) * E].rearrange("p e t -> p t e"), AX.X, ALU.add)
            then(ins)
            dve.tensor_scalar(over[:], count[:], float(C), 4.0 * NT, ALU.is_ge, ALU.mult)
            dve.scalar_tensor_tensor(out=slot[:, 0], in0=choice[:, 0], scalar=float(SLOTS), in1=count[:, 0], op0=ALU.mult, op1=ALU.add)
            then(dve.scalar_tensor_tensor(out=slot[:, 1], in0=choice[:, 1], scalar=float(SLOTS), in1=count[:, 1], op0=ALU.mult, op1=ALU.subtract))
            dve.tensor_scalar(slot[:, 0], slot[:, 0], float(SLOTS * E), None, ALU.add)
            then(dve.tensor_scalar(slot[:, 1], slot[:, 1], float(SLOTS * E + C - 1), None, ALU.add))
            then(dve.tensor_scalar(tile_f[:], slot[:], -(P - 1) / 2.0, 1.0 / P, ALU.add, ALU.mult))
            then(dve.tensor_scalar(tile_f[:], tile_f[:], ROUNDER, -ROUNDER, ALU.add, ALU.add))
            dve.scalar_tensor_tensor(out=slot_lo[:], in0=tile_f[:], scalar=-float(P), in1=slot[:], op0=ALU.mult, op1=ALU.add)
            then(dve.tensor_tensor(tile_of[:], tile_f[:], over[:], ALU.add))

            with dve.Fori(0, TILES // CH) as it:
                for k in range(TOP_K):
                    def of_chunk(row, size):
                        return cols(row, CH * it, CH).rearrange("p (o n) -> p o n", o=1).to_broadcast([P, size, CH])

                    dve.wait_ge(hot_free, 2 * it + k + 1)
                    dve.tensor_tensor(tile_hot[:, k], iota_tile[:], of_chunk(tile_of[:, k], NT), ALU.is_equal).then_inc(tile_hot_made, 1)
                    dve.tensor_tensor(slot_hot[:, k], iota_slot[:], of_chunk(slot_lo[:, k], P), ALU.is_equal)
                    dve.wait_ge(tile_hot_made, 2 * it + k + 1)
                    dve.tensor_scalar(tokens_hot[:, k, 0], tile_hot[:, k], row1[:], None, ALU.mult)
                    dve.tensor_tensor(tokens_hot[:, k, 1], tile_hot[:, k], of_chunk(tile_no, NT), ALU.mult).then_inc(hot_made, 1)

            dve.wait_ge(table_made, 1)
            then(dve.tensor_copy(table[:].rearrange("p k a c -> p (k a c)"), ps_table[:, 0:4 * NT]))
            then(dve.scalar_tensor_tensor(out=table0[:], in0=table[:, :, 1], scalar=float(P), in1=table[:, :, 0], op0=ALU.mult, op1=ALU.add))
            then(dve.scalar_tensor_tensor(out=table1[:], in0=table0[:, 0], scalar=0.0, in1=table0[:, 1], op0=ALU.is_equal, op1=ALU.mult))
            then(dve.tensor_tensor(table1[:], table1[:], table0[:, 0], ALU.add))
            then(dve.scalar_tensor_tensor(out=table2[:], in0=table1[:], scalar=0.0, in1=trash[:], op0=ALU.is_equal, op1=ALU.mult))
            dve.scalar_tensor_tensor(out=slot_token[:], in0=table1[:], scalar=-1.0, in1=table2[:], op0=ALU.add, op1=ALU.add).then_inc(slots_ready, 1)

            def input_low(it, u):
                unit, N, ring = BODY * it + u, unit_cols(u), u % 3
                e = 2 * it + u // UE
                for k in range(KD):
                    dve.wait_ge(in_hi_made, KD * unit + k + 1)
                    dve.tensor_tensor(in_lo[u % 2][:, k, 0:N], ps_turn[k][:, 0:N], in_hi[u % 2][:, k, 0:N].bitcast(F32), ALU.subtract).then_inc(in_lo_made, 1)
                gate = gathered[:, ring, :, D + e:D + e + 1] if isinstance(e, int) else gathered[:, ring, :, bass.ds(D + e, 1)]
                dve.wait_ge(y_ready, upto(UT * (unit - 2) + 1))
                dve.tensor_copy(gate_of[:, ring], gate.rearrange("p j o -> p (j o)")).then_inc(gate_copied, 1)

            def hidden_parts(it, u):
                unit, N = BODY * it + u, unit_cols(u)
                dve.wait_ge(down_made, upto(UT * (unit - 1) + 1))

                def low(c):
                    chunk = HC * u + c
                    dve.wait_ge(h_hi_made, HC * unit + c + 1)
                    dve.tensor_tensor(h_lo[u % 2][:, c, 0:N], h_f32[:, chunk % 3, 0:N], h_hi[u % 2][:, c, 0:N].bitcast(F32), ALU.subtract).then_inc(h_lo_made, 1)

                for c in range(HC):
                    chunk = HC * u + c
                    dve.wait_ge(gelu_made, HC * unit + c + 1)
                    dve.tensor_copy(h_hi[u % 2][:, c, 0:N], h_f32[:, chunk % 3, 0:N]).then_inc(h_hi_made, 1)
                    if c:
                        low(c - 1)
                low(HC - 1)

            input_low(0, 0)
            hidden_parts(0, 0)
            input_low(0, 1)

            def step3(it, u, last):
                unit, par = BODY * it + u, (u // UE) % 2
                if not last or u + 1 < BODY:
                    hidden_parts(it, u + 1)
                if not last or u + 2 < BODY:
                    input_low(it, u + 2)
                if u % UE == 0:
                    dve.wait_ge(b2_in[par], 16 * (it + 1))
                dve.wait_ge(y_added, 16 * (UT * unit + 1))
                for j in range(UT):
                    m, tile = tile_rows(u, j), UT * unit + j
                    dve.wait_ge(down_made, tile + 2)
                    dve.tensor_tensor(y_sum[0:m, j], ps_y[j][0:m, 0:D], b2_wide[0:m, par], ALU.add).then_inc(y_summed, 1)
                    dve.wait_ge(y_summed, tile + 2)
                    dve.tensor_scalar(y_out[0:m, j], y_sum[0:m, j], gate_of[0:m, u % 3, j:j + 1], None, ALU.mult).then_inc(y_ready, 1)

            steps_of_part3(dve, step3)

        @block.tensor
        def _(pe):

            for begun in (up_made, down_made):
                pe.sem_inc(begun, 1)
            pe.sem_inc(hot_free, 2)

            pe.wait_ge(attn_in, 16 * 10)
            pe.wait_ge(consts, 1)
            for n in range(2):
                pe.transpose(bank[0][:, n * P:(n + 1) * P], ctx_sb[:, n, 0:P], ident[:])
                ins = pe.transpose(bank[0][0:CR, B * KEYS + n * P:B * KEYS + (n + 1) * P], ctx_sb[:, n, P:CD], ident[:])
            ins.then_inc(prep_pe, 1)
            for i in range(KD):
                for h in range(KD):
                    ins = pe.transpose(bank[1][:, h * D + i * P:h * D + (i + 1) * P], wq_sb[:, i, h * P:(h + 1) * P], ident[:])
            ins.then_inc(prep_pe, 1)
            for h in range(KD):
                pe.transpose(bank[3][:, h * CD:h * CD + P], wv_sb[:, 0, h * P:(h + 1) * P], ident[:])
                ins = pe.transpose(bank[3][:, h * CD + P:(h + 1) * CD], wv_sb[0:CR, 1, h * P:(h + 1) * P], ident[0:CR, 0:CR])
            ins.then_inc(prep_pe, 1)
            pe.wait_ge(prep_dve, 6)
            for h in range(KD):
                to = bank[2][:, h * D:h * D + B * KEYS]
                pe.matmul(to, wk_sb[:, 0, h * P:(h + 1) * P], ctxT[:, 0, :], start=True, stop=False)
                ins = pe.matmul(to, wk_sb[0:CR, 1, h * P:(h + 1) * P], ctxT[0:CR, 1, :], start=False, stop=True)
            ins.then_inc(prep_pe, 1)
            pe.wait_ge(b1_in, 16)
            pe.wait_ge(prep_dve, 11)
            pe.transpose(bank[0][:, 0:E * HC], b1_sb[:], ident[0:E * HC, 0:E * HC])
            for k in range(KD):
                ins = pe.transpose(bank[0][:, E * HC + k * E:E * HC + (k + 1) * E], wg_mid[:, k * P:(k + 1) * P], ident[0:E, 0:E])
            ins.then_inc(prep_pe, 1)
            pe.wait_ge(prep_dve, 13)
            for i in range(KD):
                for h in range(KD):
                    pe.matmul(bank[5][:, i * D:(i + 1) * D], wqT[:, h, i * P:(i + 1) * P], keyT[:, h, :], start=(h == 0), stop=(h == KD - 1))
            for h in range(KD):
                ins = pe.matmul(bank[6][:, 0:B * KEYS], bq_wide[:, h, :], keyT[:, h, :], start=(h == 0), stop=(h == KD - 1))
            ins.then_inc(prep_pe, 1)
            pe.wait_ge(prep_dve, 15)
            for h in range(KD):
                pe.matmul(bank[4][:, 0:E], wvT[:, h, 0:P], wgT[:, h, :], start=(h == 0), stop=(h == KD - 1))
            for h in range(KD):
                pe.matmul(bank[4][0:CR, E:2 * E], wvT[:, h, P:CD], wgT[:, h, :], start=(h == 0), stop=(h == KD - 1))
            for h in range(KD):
                ins = pe.matmul(bank[4][:, 2 * E:3 * E], bv_wide[:, h, :], wgT[:, h, :], start=(h == 0), stop=(h == KD - 1))
            ins.then_inc(prep_pe, 1)
            pe.wait_ge(prep_dve, 17)
            for k in range(KD):
                ins = pe.matmul(bank[7][:, 0:B * KEYS], mean_w[:], a_raw[:, k, :], start=(k == 0), stop=(k == KD - 1))
            ins.then_inc(prep_pe, 1)

            def values():
                pe.wait_ge(prep_dve, 23)
                pe.wait_ge(prep_act, 2)
                for b in range(B):
                    to = bank[(5, 6, 7, 3)[b]][:, 0:ROW]
                    pe.matmul(to, ctxT_twice[:, 0, b].rearrange("p o k -> p (o k)"), wv_sb[:, 0, :], start=True, stop=False)
                    ins = pe.matmul(to, ctxT_twice[0:CR, 1, b].rearrange("p o k -> p (o k)"), wv_sb[0:CR, 1, :], start=False, stop=True)
                ins.then_inc(prep_pe, 1)

            def step1(it, j, on):
                pair = 4 * it + j
                if on[1]:
                    r, start = (j - 1) % 2, KG * it + KG * ((j - 1) // 4)
                    pe.wait_ge(xT_copied, pair)
                    pe.wait_ge(scores_read, upto(pair - 1))
                    pe.wait_ge(xg_copied, upto(pair - 1))
                    for t in range(2):
                        for k in range(KD):
                            ins = pe.matmul(ps_score[:, t * KG:(t + 1) * KG], xT[:, r, k, t * P:(t + 1) * P],
                                            cols(a_sb[:, k].rearrange("p b c -> p (b c)"), start, KG), start=(k == 0), stop=(k == KD - 1))
                    ins.then_inc(scores_made, 1)
                if on[2]:
                    r = j % 2
                    pe.wait_ge(probs_made, upto(pair - 1))
                    pe.wait_ge(pT_copied, upto(pair - 2))
                    pe.sem_inc(pe_waits, 1)
                    pe.transpose(ps_pT[:, 0:P], prob[:, r].rearrange("p t k -> p (t k)"), ident[:]).then_inc(pT_made, 1)
                if on[0]:
                    pe.wait_ge(x_in[j % 4], 16 * (it + 1))
                    pe.wait_ge(xT_copied, pair)
                    for k in range(KD):
                        for t in range(2):
                            at = k * 2 * P + t * P
                            ins = pe.transpose(ps_xT[:, at:at + P], x_sb[:, j % 4, t, k * P:(k + 1) * P], ident[:])
                    ins.then_inc(xT_made, 1)
                    if isinstance(it, int) and it == 0 and j == 1:
                        values()
                if on[2]:
                    r = j % 2
                    v = v_first if j == 2 else v_rest
                    if j == 2:
                        pe.wait_ge(v_first_made, it + 1)
                    if j == 3:
                        pe.wait_ge(v_rest_made, it + 1)
                    pe.wait_ge(pT_copied, upto(pair - 1))
                    pe.wait_ge(x1_made, upto(pair - 2))
                    pe.sem_inc(pe_waits, 1)
                    for t in range(2):
                        half = slice(t * KEYS, (t + 1) * KEYS)
                        ins = pe.matmul(ps_att[t][:, 0:ROW], pT[half, r, :], v[half], start=True, stop=True)
                    ins.then_inc(att_made, 1)

            pe.wait_ge(prep_dve, 23)
            steps_of_part1(pe, step1)

            pe.wait_ge(route, 11)
            moving = hot[:].rearrange("p k t e -> p k e t")
            for k in range(TOP_K):
                half = slice(k * E * TILES, (k + 1) * E * TILES)
                pe.matmul(ps_total[:, half], ones_bf[:], moving[:, k], start=True, stop=True)
                ins = pe.matmul(ps_prefix[:, half], before[:], moving[:, k], start=True, stop=True)
            ins.then_inc(counts_made, 1)
            pe.matmul(ps_table[:, 0:4 * NT], zeros_bf[:, 0:P], zeros_bf[:], start=True, stop=False, skip_group_check=True)
            with pe.Fori(0, TILES // CH) as it:
                for k in range(TOP_K):
                    tokens = tokens_hot[:, k].rearrange("p a c n -> p n (a c)")
                    pe.wait_ge(hot_made, 2 * it + k + 1)
                    for n in range(CH):
                        ins = pe.matmul(ps_table[:, 2 * k * NT:2 * (k + 1) * NT], slot_hot[:, k, :, n], tokens[:, n], start=False, stop=False, skip_group_check=True)
                    ins.then_inc(hot_free, 1)
            pe.matmul(ps_table[:, 0:4 * NT], zeros_bf[:, 0:P], zeros_bf[:], start=False, stop=True, skip_group_check=True).then_inc(table_made, 1)

            def turn(it, u):
                unit, ring = BODY * it + u, u % 3
                pe.wait_ge(rows_in[ring], 16 * UT * (2 * it + u // 3 + 1))
                pe.wait_ge(in_lo_made, KD * unit)
                for k in range(KD):
                    for j in range(UT):
                        m = tile_rows(u, j)
                        ins = pe.transpose(ps_turn[k][:, j * P:j * P + m], gathered[0:m, ring, j, k * P:(k + 1) * P], ident[0:m, 0:m])
                ins.then_inc(turned, 1)

            def up(it, u):
                unit, N, e, par = BODY * it + u, unit_cols(u), 2 * it + u // UE, (u // UE) % 2
                pe.wait_ge(in_hi_made, KD * (unit + 1))
                pe.wait_ge(in_lo_made, KD * (unit + 1))
                if u % UE == 0:
                    pe.wait_ge(w1_hi_made, 4 * e + 4)
                    pe.wait_ge(w1_lo_made, 4 * e + 4)
                for c in range(HC):
                    chunk, cut = HC * u + c, slice(c * P, (c + 1) * P)
                    to = ps_up[chunk % 3][:, 0:N]
                    pe.wait_ge(gelu_made, upto(HC * unit + c - 2))
                    for k in range(KD):
                        hi, lo = in_hi[u % 2][:, k, 0:N], in_lo[u % 2][:, k, 0:N]
                        pe.matmul(to, w1_hi[par][:, k, cut], hi, start=(k == 0), stop=False)
                        pe.matmul(to, w1_hi[par][:, k, cut], lo, start=False, stop=False)
                        ins = pe.matmul(to, w1_lo[par][:, k, cut], hi, start=False, stop=(k == KD - 1))
                    ins.then_inc(up_made, 1)

            def down(it, u):
                unit, e, par = BODY * it + u, 2 * it + u // UE, (u // UE) % 2
                pe.wait_ge(y_summed, UT * unit + 1)
                if u % UE == 0:
                    pe.wait_ge(w2_hi_made, 4 * e + 4)
                    pe.wait_ge(w2_lo_made, 4 * e + 4)
                for j in range(UT):
                    m = tile_rows(u, j)
                    to = ps_y[j][0:m, 0:D]
                    for c in range(HC):
                        if j == 0:
                            pe.wait_ge(h_lo_made, HC * unit + c + 1)
                        hi, lo = (h[u % 2][:, c, j * P:j * P + m] for h in (h_hi, h_lo))
                        pe.matmul(to, hi, w2_hi[par][:, c, :], start=(c == 0), stop=False)
                        pe.matmul(to, hi, w2_lo[par][:, c, :], start=False, stop=False)
                        ins = pe.matmul(to, lo, w2_hi[par][:, c, :], start=False, stop=(c == HC - 1))
                    ins.then_inc(down_made, 1)

            turn(0, 0)
            up(0, 0)
            turn(0, 1)

            def step3(it, u, last):
                if not last or u + 1 < BODY:
                    up(it, u + 1)
                if not last or u + 2 < BODY:
                    turn(it, u + 2)
                down(it, u)

            steps_of_part3(pe, step3)


_INS = ["x", "ctx_768", "L0_xattn_Wq", "L0_xattn_bq", "L0_xattn_Wk", "L0_xattn_bk", "L0_xattn_Wv", "L0_xattn_bv",
        "L0_ffn_Wg", "L0_ffn_W1", "L0_ffn_b1", "L0_ffn_W2", "L0_ffn_b2"]


def kernel(**inputs):
    import numpy as _np
    import concourse.bacc as _bacc
    from concourse import mybir as _mybir
    from concourse.bass_utils import run_bass_kernel_spmd as _run

    nc = _bacc.Bacc("TRN2", target_bir_lowering=False, num_devices=1)
    arrays, args = {}, []
    for name in _INS:
        a = _np.ascontiguousarray(inputs[name])
        arrays[f"in_{name}_dram"] = a
        args.append(nc.dram_tensor(f"in_{name}_dram", a.shape, _mybir.dt.from_np(a.dtype), kind="ExternalInput").ap())
    B, S, D = inputs["x"].shape
    args.append(nc.dram_tensor("out_0_dram", (B * S + P, D), _mybir.dt.float32, kind="ExternalOutput").ap())
    xattn_moe(nc, *args)
    r = _run(nc, [arrays], core_ids=[0])
    return r.results[0]["out_0_dram"][:B * S].reshape(B, S, D)
```

```python
from contextlib import ExitStack

import concourse.bass as bass
from concourse import mybir

P = 128
F32 = mybir.dt.float32
F32R = mybir.dt.float32r
BF16 = mybir.dt.bfloat16
I32 = mybir.dt.int32
ALU = mybir.AluOpType
ACT = mybir.ActivationFunctionType
AX = mybir.AxisListType
EPS = 1e-5
ROUNDER = 12582912.0
TOP_K = 2
CAP_RATIO = 1.05


def upto(value):
    return max(value, 0) if isinstance(value, int) else value


def xattn_moe(nc, x, ctx, Wq, bq, Wk, bk, Wv, bv, Wg, W1, b1, W2, b2, out):
    B, S, D = x.shape
    T = B * S
    KEYS, CD = ctx.shape[1:]
    E, _, H = W1.shape
    C = int(round(TOP_K * T * CAP_RATIO / E))
    TILES = T // P
    PAIRS = TILES // 2
    PB = PAIRS // B
    KD = D // P
    HC = H // P
    CR = CD - P
    ST = -(-C // P)
    UT = 3
    UE = ST // UT
    LAST = (C - (ST - 1) * P + 1) // 2 * 2
    SLOTS = ST * P
    UNITS = E * UE
    BODY = 2 * UE
    ROW = D + E
    NT = E * ST
    KG = KEYS + E
    CH = 8
    EARLY = TILES - CH
    assert TILES == 4 * CH
    CHOICES = TOP_K * E
    assert KD == 2 and PB == 4 and ST % UT == 0 and UE == 3 and KEYS == 64 and P < CD <= 2 * P and TILES % 2 == 0

    with ExitStack() as stack:
        def sb(name, shape, dt=F32):
            return stack.enter_context(nc.sbuf_tensor(name, shape, dt))

        def sem(name):
            return stack.enter_context(nc.semaphore(name))

        rows_dram = nc.dram_tensor("rows_scratch", (T + P, ROW), F32).ap()

        bank = [stack.enter_context(nc.psum_tensor(f"bank{i}", [P, 512], F32)) for i in range(8)]
        ps_xT, ps_score, ps_pT, ps_att = bank[0], bank[1], bank[2], bank[3:5]
        ps_prefix, ps_total, ps_table = bank[5], bank[6], bank[7]
        ps_up, ps_turn, ps_y = bank[0:3], bank[3:5], bank[5:8]

        ident = sb("ident", [P, P])
        zeros = sb("zeros", [P, ROW])
        b1_sb = sb("b1_sb", [E * HC, P])
        b1T = sb("b1T", [P, E * HC])
        slot_token = sb("slot_token", [P, NT], I32)
        unit_token = sb("unit_token", [P, BODY, UT], I32)
        w1_raw = sb("w1_raw", [P, KD, H])
        w2_raw = sb("w2_raw", [P, HC, D])
        w1_hi = [sb(f"w1_hi{i}", [P, KD, H], F32R) for i in range(2)]
        w1_lo = [sb(f"w1_lo{i}", [P, KD, H], F32R) for i in range(2)]
        w2_hi = [sb(f"w2_hi{i}", [P, HC, D], F32R) for i in range(2)]
        w2_lo = [sb(f"w2_lo{i}", [P, HC, D], F32R) for i in range(2)]
        b2_wide = sb("b2_wide", [P, 2, D])
        gathered = sb("gathered", [P, 3, UT, ROW])

        early = ExitStack()

        def tmp(name, shape, dt=F32):
            return early.enter_context(nc.sbuf_tensor(name, shape, dt))

        iota_slot = tmp("iota_slot", [P, P, CH], BF16)
        iota_tile = tmp("iota_tile", [P, NT, CH], BF16)
        tile_no = tmp("tile_no", [P, TILES], BF16)
        iota_e8 = tmp("iota_e8", [P, TILES, E])
        row1 = tmp("row1", [P, 1])
        trash = tmp("trash", [P, NT])
        before = tmp("before", [P, P], BF16)
        ones_bf = tmp("ones_bf", [P, P], BF16)
        ones = tmp("ones", [P, P])
        zeros_bf = tmp("zeros_bf", [P, 4 * NT], BF16)
        mean_w = tmp("mean_w", [P, P])
        minus_half = tmp("minus_half", [P, 2])
        scan_keep = tmp("scan_keep", [P, CHOICES * (TILES + 1)])
        wq_sb = tmp("wq_sb", [P, KD, D])
        wk_sb = tmp("wk_sb", [P, 2, D])
        wv_sb = tmp("wv_sb", [P, 2, ROW])
        ctx_sb = tmp("ctx_sb", [P, 2, CD])
        ctxT = tmp("ctxT", [P, 2, B * KEYS])
        ctxT_twice = tmp("ctxT_twice", [P, 2, B, 2, KEYS])
        bq_sb = tmp("bq_sb", [P, KD])
        bk_sb = tmp("bk_sb", [P, KD])
        bq_wide = tmp("bq_wide", [P, KD, P])
        bv_col = tmp("bv_col", [P, KD])
        bv_wide = tmp("bv_wide", [P, KD, P])
        bv_sb = tmp("bv_sb", [P, ROW])
        wqT = tmp("wqT", [P, KD, D])
        wvT = tmp("wvT", [P, KD, CD])
        keyT = tmp("keyT", [P, KD, B * KEYS])
        a_raw = tmp("a_raw", [P, KD, B * KEYS])
        a_sb = tmp("a_sb", [P, KD, B, KG])
        c_sb = tmp("c_sb", [P, B * KEYS])
        v_sb = tmp("v_sb", [P, B, 2, ROW])
        wg_sb = tmp("wg_sb", [E, D])
        wg_mean = tmp("wg_mean", [E, 2])
        wg_mid = tmp("wg_mid", [E, D])
        wgT = tmp("wgT", [P, KD, E])
        x_sb = tmp("x_sb", [P, 4, 2, ROW])
        xT = tmp("xT", [P, 2, KD, 2 * P])
        stat1 = tmp("stat1", [P, 2, 2, 6])
        mv1 = tmp("mv1", [P, 2, 2, 2])
        var1 = tmp("var1", [P, 2, 2])
        rstd1 = tmp("rstd1", [P, 2, 2])
        score = tmp("score", [P, 2, 2, KEYS])
        nmax = tmp("nmax", [P, 2, 2])
        prob = tmp("prob", [P, 2, 2, KEYS])
        psum_row = tmp("psum_row", [P, 2, 2])
        pinv = tmp("pinv", [P, 2, 2])
        pT = tmp("pT", [P, 2, P])
        x1 = tmp("x1", [P, 2, 2, ROW])
        stat2 = tmp("stat2", [P, 2, 2, 6])
        mv2 = tmp("mv2", [P, 2, 2, 2])
        var2 = tmp("var2", [P, 2, 2])
        rstd2 = tmp("rstd2", [P, 2, 2])
        nmean2 = tmp("nmean2", [P, 2, 2])
        shift2 = tmp("shift2", [P, 2, 2])
        rows = tmp("rows", [P, 4, 2, ROW])
        gmax = tmp("gmax", [P, 2, 4])
        gsub = tmp("gsub", [P, 2, 4, E])
        gexp = tmp("gexp", [P, 2, 4, E])
        gsum = tmp("gsum", [P, 2, 4])
        ginv = tmp("ginv", [P, 2, 4])
        gates = tmp("gates", [P, TILES, E])
        best = tmp("best", [P, TOP_K, TILES])
        same = tmp("same", [P, TILES, E])
        choice = tmp("choice", [P, TOP_K, TILES])
        hot = tmp("hot", [P, TOP_K, TILES, E], BF16)
        rest = tmp("rest", [P, TILES, E])
        running = tmp("running", [P, CHOICES * (TILES + 1)])
        late_total = tmp("late_total", [P, CHOICES, CH + 1])
        place = tmp("place", [P, CHOICES, TILES])
        picked = tmp("picked", [P, CHOICES, TILES])
        count = tmp("count", [P, TOP_K, TILES])
        over = tmp("over", [P, TOP_K, TILES])
        slot = tmp("slot", [P, TOP_K, TILES])
        tile_f = tmp("tile_f", [P, TOP_K, TILES])
        slot_lo = tmp("slot_lo", [P, TOP_K, TILES], BF16)
        tile_of = tmp("tile_of", [P, TOP_K, TILES], BF16)
        slot_hot = tmp("slot_hot", [P, TOP_K, P, CH], BF16)
        tile_hot = tmp("tile_hot", [P, TOP_K, NT, CH], BF16)
        tokens_hot = tmp("tokens_hot", [P, TOP_K, 2, NT, CH], BF16)
        table = tmp("table", [P, TOP_K, 2, NT])
        table0 = tmp("table0", [P, TOP_K, NT])
        table1 = tmp("table1", [P, NT])
        table2 = tmp("table2", [P, NT])
        early.close()

        gate_of = sb("gate_of", [P, 3, UT])
        in_hi = [sb(f"in_hi{i}", [P, KD, UT * P], F32R) for i in range(2)]
        in_lo = [sb(f"in_lo{i}", [P, KD, UT * P], F32R) for i in range(2)]
        h_f32 = sb("h_f32", [P, 3, UT * P])
        h_hi = [sb(f"h_hi{i}", [P, HC, UT * P], F32R) for i in range(2)]
        h_lo = [sb(f"h_lo{i}", [P, HC, UT * P], F32R) for i in range(2)]
        y_sum = sb("y_sum", [P, UT, D])
        y_out = sb("y_out", [P, UT, D])

        ctx_in, wk_in, wq_in, wv_in = sem("ctx_in"), sem("wk_in"), sem("wq_in"), sem("wv_in")
        bq_in, b1_in, wg_in = sem("bq_in"), sem("b1_in"), sem("wg_in")
        consts = sem("consts")
        zeroed = sem("zeroed")
        filled = sem("filled")
        prep_pe = sem("prep_pe")
        ctxT_copied, ctxT_doubled, wqT_copied, key_made = sem("ctxT_copied"), sem("ctxT_doubled"), sem("wqT_copied"), sem("key_made")
        wg_centred, small_copied, bq_wide_made, bv_wide_made = sem("wg_centred"), sem("small_copied"), sem("bq_wide_made"), sem("bv_wide_made")
        a_copied, c_copied, a_centred = sem("a_copied"), sem("c_copied"), sem("a_centred")
        wvT_copied, vg_copied, values_zeroed, values_made = sem("wvT_copied"), sem("vg_copied"), sem("values_zeroed"), sem("values_made")

        pool_waits, act_waits, dve_waits, pe_waits = sem("pool_waits"), sem("act_waits"), sem("dve_waits"), sem("pe_waits")

        x_in = [sem(f"x_in{i}") for i in range(4)]
        xT_made, xT_copied, scores_made, scores_read = sem("xT_made"), sem("xT_copied"), sem("scores_made"), sem("scores_read")
        xg_copied = sem("xg_copied")
        stats1_made, mv1_made, var1_made, rstd1_made = sem("stats1_made"), sem("mv1_made"), sem("var1_made"), sem("rstd1_made")
        score_scaled = sem("score_scaled")
        probs_made, pT_made, pT_copied, att_made = sem("probs_made"), sem("pT_made"), sem("pT_copied"), sem("att_made")
        pinv_made, x1_made, stats2_made, mv2_made = sem("pinv_made"), sem("x1_made"), sem("stats2_made"), sem("mv2_made")
        var2_made, rstd2_made, shift2_made = sem("var2_made"), sem("rstd2_made"), sem("shift2_made")
        rows0_made, rows1_made = sem("rows0_made"), sem("rows1_made")
        x1_stored = [sem(f"x1_stored{i}") for i in range(2)]
        rows_stored = [sem(f"rows_stored{i}") for i in range(2)]
        gmax_made, gsub_made, gexp_made, gsum_made, ginv_made, gates_made, rows_gated = (
            sem("gmax_made"), sem("gsub_made"), sem("gexp_made"), sem("gsum_made"), sem("ginv_made"),
            sem("gates_made"), sem("rows_gated"))

        route = sem("route")
        counts_made = sem("counts_made")
        token_rows_made = sem("token_rows_made")
        tile_hot_made, hot_made, hot_free = sem("tile_hot_made"), sem("hot_made"), sem("hot_free")
        table_made, slots_ready = sem("table_made"), sem("slots_ready")

        w1_in, w2_in = sem("w1_in"), sem("w2_in")
        b2_in = [sem("b2_in0"), sem("b2_in1")]
        w1_hi_made, w1_lo_made, w2_hi_made, w2_lo_made = sem("w1_hi_made"), sem("w1_lo_made"), sem("w2_hi_made"), sem("w2_lo_made")
        rows_in = [sem(f"rows_in{i}") for i in range(3)]
        unit_token_made, gate_copied = sem("unit_token_made"), sem("gate_copied")
        turned, in_hi_made, in_lo_made = sem("turned"), sem("in_hi_made"), sem("in_lo_made")
        up_made, gelu_made, h_hi_made, h_lo_made = sem("up_made"), sem("gelu_made"), sem("h_hi_made"), sem("h_lo_made")
        down_made, y_summed, y_ready, y_added = sem("down_made"), sem("y_summed"), sem("y_ready"), sem("y_added")

        x_pairs = x.rearrange("b s d -> (b s) d").rearrange("(n t p) d -> n p t d", t=2, p=P)
        out_pairs = out[0:T, :].rearrange("(n t p) d -> n p t d", t=2, p=P)
        rows_batches = rows_dram[0:T, :].rearrange("(n t p) d -> n p t d", t=4, p=P)
        w1_view = W1.rearrange("e (k p) h -> e p k h", p=P)
        w2_view = W2.rearrange("e (c p) d -> e p c d", p=P)

        def one(view, i):
            if isinstance(i, int):
                return view[i]
            names = "abc"[:len(view.shape) - 1]
            return view[bass.ds(i, 1)].rearrange(f"o {' '.join(names)} -> (o {names[0]}) {' '.join(names[1:])}")

        def cols(ap, start, size):
            return ap[:, start:start + size] if isinstance(start, int) else ap[:, bass.ds(start, size)]

        def steps_of_part1(eng, step):
            for s in range(PB):
                step(0, s, [s - lag >= 0 for lag in range(5)])
            with eng.Fori(1, PAIRS // PB) as it:
                for j in range(PB):
                    step(it, j, [True] * 5)
            for s in range(PAIRS, PAIRS + PB):
                step(PAIRS // PB, s - PAIRS, [s - lag < PAIRS for lag in range(5)])

        def gates_due(it, j):
            return j % 2 == 1 and not (isinstance(it, int) and it == 0)

        def gate_batch(it, j):
            return 2 * it + (j - 3) // 2

        def steps_of_part3(eng, step):
            with eng.Fori(0, UNITS // BODY - 1) as it:
                for u in range(BODY):
                    step(it, u, False)
            for u in range(BODY):
                step(UNITS // BODY - 1, u, True)

        def scan_rows(buf):
            at = CHOICES * EARLY
            return ((buf[:, 0:at].rearrange("p (m t) -> p m t", m=CHOICES), EARLY),
                    (buf[:, at:at + CHOICES * (CH + 1)].rearrange("p (m t) -> p m t", m=CHOICES), CH + 1))

        def count_cols(ps, late):
            at = CHOICES * EARLY
            return ps[:, at:at + CHOICES * CH] if late else ps[:, 0:at]

        def tile_rows(u, j):
            return LAST if u % UE == UE - 1 and j == UT - 1 else P

        def unit_cols(u):
            return (UT - 1) * P + tile_rows(u, UT - 1)

        value_batches = ((), (0,), (1,), (2, 3))
        assert B == 4
        routed = []
        block = stack.enter_context(nc.Block())

        @block.sync
        def _(sp):
            def load_x(pair, ring):
                sp.dma_start(x_sb[:, ring, :, 0:D], one(x_pairs, pair)).then_inc(x_in[ring], 16)

            sp.dma_start(ctx_sb[:], ctx.rearrange("b k c -> (b k) c").rearrange("(n p) c -> p n c", p=P)).then_inc(ctx_in, 16)
            sp.dma_start(wk_sb[:, 0, 0:D], Wk[0:P, :]).then_inc(wk_in, 16)
            sp.dma_start(wk_sb[0:CR, 1, 0:D], Wk[P:CD, :]).then_inc(wk_in, 16)
            sp.dma_start(wq_sb[:], Wq.rearrange("(k p) h -> p k h", p=P)).then_inc(wq_in, 16)
            with nc.allow_non_contiguous_dma(reason="two columns of 128 biases"):
                sp.dma_start(bk_sb[:], bk.rearrange("(k p) -> p k", p=P)).then_inc(wk_in, 16)
                sp.dma_start(bq_sb[:], bq.rearrange("(k p) -> p k", p=P)).then_inc(bq_in, 16)
                sp.dma_start(bv_col[:], bv.rearrange("(k p) -> p k", p=P)).then_inc(wv_in, 16)
            sp.dma_start(wg_sb[:], Wg).then_inc(wg_in, 16)
            sp.dma_start(b1_sb[:], b1.rearrange("e (c p) -> (e c) p", p=P)).then_inc(b1_in, 16)
            load_x(0, 0)
            sp.dma_start(wv_sb[:, 0, 0:D], Wv[0:P, :]).then_inc(wv_in, 16)
            sp.dma_start(wv_sb[0:CR, 1, 0:D], Wv[P:CD, :]).then_inc(wv_in, 16)
            sp.dma_start(bv_sb[:, 0:D], bv.rearrange("(o d) -> o d", o=1).to_broadcast([P, D])).then_inc(wv_in, 16)
            sp.wait_ge(zeroed, 1)
            quarter = P // 4
            for i, stored in enumerate(x1_stored + rows_stored):
                sp.dma_start(rows_dram[T + i * quarter:T + (i + 1) * quarter, :], zeros[0:quarter, :]).then_inc(stored, 16)

            def load_w1(e):
                sp.dma_start(w1_raw[:], one(w1_view, e)).then_inc(w1_in, 16)

            def load_w2(e):
                sp.dma_start(w2_raw[:], one(w2_view, e)).then_inc(w2_in, 16)

            def load_b2(e, ring):
                sp.dma_start(b2_wide[:, ring], (b2[e:e + 1] if isinstance(e, int) else b2[bass.ds(e, 1)]).to_broadcast([P, D])).then_inc(b2_in[ring], 16)

            def step1(it, j, on):
                pair = 4 * it + j
                if on[0] and not (isinstance(it, int) and pair == 0):
                    sp.wait_ge(x1_made, upto(pair - 3))
                    load_x(pair, j)
                if on[4]:
                    sp.wait_ge(x1_made, pair - 3)
                    sp.dma_start(one(out_pairs, pair - 4), x1[:, j % 2, :, 0:D]).then_inc(x1_stored[j % 2], 16)
                if isinstance(it, int) and it == 0 and j == 3:
                    load_w1(0)
                    load_w2(0)
                    load_b2(0, 0)

            steps_of_part1(sp, step1)

            def step3(it, u, last):
                e = 2 * it + u // UE
                if last and u >= UE:
                    return
                if u % UE == 0:
                    sp.wait_ge(w1_hi_made, 4 * e + 4)
                    sp.wait_ge(w1_lo_made, 4 * e + 4)
                    load_w1(e + 1)
                    sp.wait_ge(w2_hi_made, 4 * e + 4)
                    sp.wait_ge(w2_lo_made, 4 * e + 4)
                    load_w2(e + 1)
                    sp.wait_ge(y_summed, UT * UE * e + 1)
                    load_b2(e + 1, (u // UE + 1) % 2)

            steps_of_part3(sp, step3)
            sp.wait_ge(y_added, 16 * (UT * UNITS + 1))

        @block.gpsimd
        def _(pool):

            n = 0

            def const(ins):
                nonlocal n
                n += 1
                ins.then_inc(consts, 1)

            small = dict(allow_small_or_imprecise_dtypes=True)
            pool.sem_inc(rows0_made, 1)
            pool.wait_ge(zeroed, 2)
            pool.dma_start(out[T:T + P, :], zeros[:, 0:D]).then_inc(y_added, 16)
            const(pool.affine_select(out=ident[:], in_=ones[:], compare_op=ALU.is_equal, fill=0.0, base=0, pattern=[[-1, P]], channel_multiplier=1))
            const(pool.memset(minus_half[:], -0.5))
            const(pool.iota(iota_slot[:], [[1, P], [0, CH]], base=0, channel_multiplier=0, **small))
            const(pool.iota(iota_tile[:], [[1, NT], [0, CH]], base=0, channel_multiplier=0, **small))
            const(pool.iota(tile_no[:], [[1, TILES]], base=0, channel_multiplier=0, **small))
            const(pool.iota(iota_e8[:], [[0, TILES], [1, E]], base=-E, channel_multiplier=0, **small))
            const(pool.iota(row1[:], [[0, 1]], base=1, channel_multiplier=1, **small))
            const(pool.iota(trash[:], [[0, NT]], base=T + 1, channel_multiplier=1, **small))
            const(pool.memset(ones_bf[:], 1.0))
            pool.memset(before[:], -1.0).then_inc(filled, 1)
            pool.memset(scan_keep[:], 1.0).then_inc(filled, 1)
            pool.wait_ge(filled, 1)
            const(pool.affine_select(out=before[:], in_=before[:], compare_op=ALU.is_ge, fill=0.0, base=0, pattern=[[-1, P]], channel_multiplier=1))
            pool.wait_ge(filled, 2)
            for keep, n_tiles in scan_rows(scan_keep):
                const(pool.affine_select(out=keep, in_=keep, compare_op=ALU.is_gt, fill=0.0, base=0, pattern=[[0, CHOICES], [1, n_tiles]], channel_multiplier=0))
            pool.memset(v_sb[:], 0.0).then_inc(values_zeroed, 1)
            const(pool.memset(gathered[:], 0.0))
            pool.wait_ge(consts, n)

            def step1(it, j, on):
                pair = 4 * it + j
                if on[0]:
                    r = j % 2
                    pool.wait_ge(mv1_made, pair + 1)
                    pool.wait_ge(score_scaled, upto(pair - 1))
                    pool.sem_inc(pool_waits, 1)
                    pool.tensor_scalar(var1[:, r], mv1[:, r, :, 1], 1.0, EPS, ALU.mult, ALU.add).then_inc(var1_made, 1)
                    pool.wait_ge(var1_made, pair + 1)
                    pool.tensor_tensor(rstd1[:, r], var1[:, r], minus_half[:], ALU.pow).then_inc(rstd1_made, 1)
                if on[3]:
                    r, ring = (j - 3) % 2, (j - 3) % 4
                    pool.wait_ge(mv2_made, pair - 2)
                    pool.wait_ge(rows1_made, upto(pair - 3))
                    pool.sem_inc(pool_waits, 1)
                    pool.tensor_scalar(var2[:, r], mv2[:, r, :, 1], 1.0, EPS, ALU.mult, ALU.add)
                    pool.tensor_scalar(nmean2[:, r], mv2[:, r, :, 0], -1.0, 0.0, ALU.mult, ALU.add).then_inc(var2_made, 1)
                    pool.wait_ge(var2_made, pair - 2)
                    pool.tensor_tensor(rstd2[:, r], var2[:, r], minus_half[:], ALU.pow).then_inc(rstd2_made, 1)
                    pool.wait_ge(rstd2_made, pair - 2)
                    pool.tensor_tensor(shift2[:, r], nmean2[:, r], rstd2[:, r], ALU.mult).then_inc(shift2_made, 1)
                    pool.wait_ge(shift2_made, pair - 2)
                    pool.wait_ge(rows_stored[ring // 2], 16 * (it + (j - 3) // 4 + 1))
                    pool.sem_inc(pool_waits, 1)
                    pool.tensor_scalar(rows[:, ring, 0], x1[:, r, 0], rstd2[:, r, 0:1], shift2[:, r, 0:1], ALU.mult, ALU.add).then_inc(rows0_made, 1)

            steps_of_part1(pool, step1)

            def w1_low(e, par):
                w1h, w1l, raw = (a[:].rearrange("p k (b h) -> p (k b) h", b=2) for a in (w1_hi[par], w1_lo[par], w1_raw))
                for b in range(4):
                    pool.wait_ge(w1_hi_made, 4 * e + b + 1)
                    pool.tensor_tensor(w1l[:, b], raw[:, b], w1h[:, b].bitcast(F32), ALU.subtract).then_inc(w1_lo_made, 1)

            def w2_low(e, par):
                w2h, w2l, raw = (a[:].rearrange("p (b c) d -> p b (c d)", b=4) for a in (w2_hi[par], w2_lo[par], w2_raw))
                for b in range(4):
                    pool.wait_ge(w2_hi_made, 4 * e + b + 1)
                    pool.tensor_tensor(w2l[:, b], raw[:, b], w2h[:, b].bitcast(F32), ALU.subtract).then_inc(w2_lo_made, 1)

            pool.wait_ge(w1_in, 16)
            w1_low(0, 0)
            pool.wait_ge(w2_in, 16)
            w2_low(0, 0)

            def gather(it, u):
                ring, index = u % 3, u % BODY
                unit = BODY * it + u
                pool.tensor_copy(unit_token[:, index], cols(slot_token, UT * unit, UT)).then_inc(unit_token_made, 1)
                pool.wait_ge(unit_token_made, unit + 1)
                pool.sem_inc(pool_waits, 1)
                for j in range(UT):
                    n_rows = tile_rows(u, j)
                    pool.indirect_dma_start(
                        gathered[0:n_rows, ring, j, :], None, rows_dram[:, :],
                        bass.IndirectOffsetOnAxis(ap=unit_token[0:n_rows, index, j:j + 1], axis=0),
                    ).then_inc(rows_in[ring], 16)

            for ring in range(2):
                pool.wait_ge(rows_stored[ring], 16 * (PAIRS // 4 + 1))
            for ring in range(2):
                pool.wait_ge(x1_stored[ring], 16 * (PAIRS // 2 + 1))
            pool.wait_ge(slots_ready, 1)
            for u in range(3):
                gather(0, u)

            def step3(it, u, last):
                unit = BODY * it + u
                e = 2 * it + u // UE
                par = (u // UE + 1) % 2
                if not last or u + 3 < BODY:
                    pool.wait_ge(turned, unit + 1)
                    pool.wait_ge(gate_copied, unit + 1)
                    gather(it, u + 3)
                if not last or u < UE:
                    if u % UE == 0:
                        w1_low(e + 1, par)
                    if u % UE == 1:
                        w2_low(e + 1, par)
                for j in range(UT):
                    n_rows, tile = tile_rows(u, j), UT * unit + j
                    pool.wait_ge(y_ready, tile + 2)
                    pool.wait_ge(y_added, 16 * (tile + 1))
                    pool.sem_inc(pool_waits, 1)
                    pool.indirect_dma_start(
                        out[:, :], bass.IndirectOffsetOnAxis(ap=unit_token[0:n_rows, u, j:j + 1], axis=0),
                        y_out[0:n_rows, j, :], None, compute_op=ALU.add,
                    ).then_inc(y_added, 16)

            steps_of_part3(pool, step3)

        @block.scalar
        def _(act):

            act.sem_inc(rows1_made, 1)

            act.wait_ge(ctxT_copied, 2)
            for n, part in ((0, P), (1, CR)):
                act.copy(ctxT_twice[0:part, n], ctxT[0:part, n, :].rearrange("p (b o k) -> p b o k", b=B, o=1).to_broadcast([part, B, 2, KEYS])).then_inc(ctxT_doubled, 1)

            def w1_high(e, par, b):
                w1h, raw = (a[:].rearrange("p k (b h) -> p (k b) h", b=2) for a in (w1_hi[par], w1_raw))
                act.copy(w1h[:, b], raw[:, b]).then_inc(w1_hi_made, 1)

            def w2_high(e, par, b):
                w2h, raw = (a[:].rearrange("p (b c) d -> p b (c d)", b=4) for a in (w2_hi[par], w2_raw))
                act.copy(w2h[:, b], raw[:, b]).then_inc(w2_hi_made, 1)

            def token_rows(chunk):
                for k in range(TOP_K):
                    act.wait_ge(tile_hot_made, 2 * chunk + k + 1)
                    act.wait_ge(hot_free, 2 * chunk + k + 1)
                    act.activation(tokens_hot[:, k, 0], tile_hot[:, k], ACT.Copy, scale=row1[:]).then_inc(token_rows_made, 1)

            def step1(it, j, on):
                pair = 4 * it + j
                if on[2]:
                    r = j % 2
                    act.wait_ge(pT_made, upto(pair - 1))
                    act.wait_ge(att_made, upto(pair - 3))
                    act.copy(pT[:, r], ps_pT[:, 0:P]).then_inc(pT_copied, 1)
                if on[0]:
                    r = j % 2
                    act.wait_ge(xT_made, pair + 1)
                    act.wait_ge(scores_made, upto(pair - 1))
                    act.copy(xT[:, r], ps_xT[:].rearrange("p (k t) -> p k t", k=KD)).then_inc(xT_copied, 1)
                if on[1]:
                    act.wait_ge(scores_read, pair)
                    act.copy(x_sb[:, (j - 1) % 4, :, D:ROW], ps_score[:, 0:2 * KG].rearrange("p (t c) -> p t c", t=2)[:, :, KEYS:KG]).then_inc(xg_copied, 1)
                if on[4]:
                    r = j % 2
                    act.wait_ge(shift2_made, pair - 3)
                    act.wait_ge(rows_stored[j // 2], 16 * it)
                    act.sem_inc(act_waits, 1)
                    act.activation(rows[:, j, 1], x1[:, r, 1], ACT.Identity, scale=rstd2[:, r, 1:2], bias=shift2[:, r, 1:2]).then_inc(rows1_made, 1)
                if gates_due(it, j):
                    act.wait_ge(gsub_made, gate_batch(it, j))
                    act.activation(gexp[:, j // 2], gsub[:, j // 2], ACT.Exp).then_inc(gexp_made, 1)
                if on[1]:
                    r = (j - 1) % 2
                    act.wait_ge(score_scaled, pair)
                    act.wait_ge(pT_made, upto(pair - 2))
                    act.wait_ge(pinv_made, upto(pair - 2))
                    for t in range(2):
                        ins = act.activation(prob[:, r, t], score[:, r, t], ACT.Exp, bias=nmax[:, r, t:t + 1], accum_out=psum_row[:, r, t:t + 1])
                    ins.then_inc(probs_made, 1)
                if isinstance(it, int) and it == PAIRS // PB:
                    if j == 0:
                        act.wait_ge(w1_in, 16)
                        for b in range(4):
                            w1_high(0, 0, b)
                    if j == 1:
                        act.wait_ge(w2_in, 16)
                        for b in range(4):
                            w2_high(0, 0, b)
                    if j == 2:
                        token_rows(0)
                if gates_due(it, j):
                    act.wait_ge(rows_gated, gate_batch(it, j))
                    act.dma_start(one(rows_batches, gate_batch(it, j) - 1), rows[:, j - 1:j + 1].rearrange("p n t d -> p (n t) d")).then_inc(rows_stored[j // 2], 16)

            steps_of_part1(act, step1)
            for chunk in range(1, TILES // CH):
                token_rows(chunk)


            def input_high(it, u):
                unit, N = BODY * it + u, unit_cols(u)
                for k in range(KD):
                    act.wait_ge(turned, unit + 1)
                    act.wait_ge(up_made, upto(HC * (unit - 1) + 1))
                    act.copy(in_hi[u % 2][:, k, 0:N], ps_turn[k][:, 0:N]).then_inc(in_hi_made, 1)

            def gelu(it, u, c):
                unit, N = BODY * it + u, unit_cols(u)
                e, chunk = 2 * it + u // UE, HC * u + c
                n = HC * unit + c
                act.wait_ge(up_made, n + 2)
                act.wait_ge(h_lo_made, upto(n - 2))
                act.sem_inc(act_waits, 1)
                act.activation(h_f32[:, chunk % 3, 0:N], ps_up[chunk % 3][:, 0:N], ACT.Gelu, bias=cols(b1T, HC * e + c, 1)).then_inc(gelu_made, 1)

            act.wait_ge(small_copied, 3)
            input_high(0, 0)
            for c in range(HC):
                if c == HC // 2:
                    input_high(0, 1)
                gelu(0, 0, c)

            def step3(it, u, last):
                unit = BODY * it + u
                e, par = 2 * it + u // UE, (u // UE + 1) % 2
                for c in range(HC):
                    if not last or u + 1 < BODY:
                        gelu(it, u + 1, c)
                    if c % 2 == 1 and (not last or u < UE):
                        if u % UE == 0:
                            act.wait_ge(w1_in, 16 * (e + 2))
                            act.wait_ge(up_made, HC * unit + 1)
                            w1_high(e + 1, par, c // 2)
                        if u % UE == 1:
                            act.wait_ge(w2_in, 16 * (e + 2))
                            act.wait_ge(down_made, upto(UT * (unit - 1) + 1))
                            w2_high(e + 1, par, c // 2)
                if not last or u + 2 < BODY:
                    input_high(it, u + 2)

            steps_of_part3(act, step3)

        @block.vector
        def _(dve):

            for begun in (y_summed, y_ready):
                dve.sem_inc(begun, 1)

            dve.memset(zeros[:], 0.0).then_inc(zeroed, 1)
            dve.memset(ones[:], 1.0).then_inc(zeroed, 1)
            dve.memset(mean_w[:], 1.0 / D).then_inc(zeroed, 1)
            dve.memset(zeros_bf[:], 0.0).then_inc(zeroed, 1)
            dve.wait_ge(zeroed, 4)

            dve.wait_ge(prep_pe, 1)
            dve.tensor_copy(ctxT[:, 0, :], bank[0][:, 0:B * KEYS]).then_inc(ctxT_copied, 1)
            dve.tensor_copy(ctxT[0:CR, 1, :], bank[0][0:CR, B * KEYS:2 * B * KEYS]).then_inc(ctxT_copied, 1)
            dve.wait_ge(bq_in, 16)
            for k in range(KD):
                dve.tensor_scalar(bq_wide[:, k, :], ones[:], bq_sb[:, k:k + 1], None, ALU.mult).then_inc(bq_wide_made, 1)
            dve.wait_ge(prep_pe, 2)
            dve.tensor_copy(wqT[:], bank[1][:].rearrange("p (k i) -> p k i", k=KD)).then_inc(wqT_copied, 1)
            dve.wait_ge(wg_in, 16)
            dve.tensor_reduce(wg_mean[:, 0:1], wg_sb[:], AX.X, ALU.add).then_inc(wg_centred, 1)
            dve.wait_ge(wg_centred, 1)
            dve.tensor_scalar(wg_mean[:, 1:2], wg_mean[:, 0:1], 1.0 / D, None, ALU.mult).then_inc(wg_centred, 1)
            dve.wait_ge(wg_centred, 2)
            dve.tensor_scalar(wg_mid[:], wg_sb[:], wg_mean[:, 1:2], None, ALU.subtract).then_inc(wg_centred, 1)
            dve.wait_ge(prep_pe, 3)
            dve.wait_ge(wk_in, 48)
            for k in range(KD):
                dve.tensor_scalar(keyT[:, k], bank[2][:, k * D:(k + 1) * D], bk_sb[:, k:k + 1], float(D) ** -0.5, ALU.add, ALU.mult).then_inc(key_made, 1)
            dve.wait_ge(prep_pe, 4)
            dve.tensor_copy(b1T[:], bank[0][:, 0:E * HC]).then_inc(small_copied, 1)
            g_ps = bank[0][:, E * HC:E * HC + KD * E]
            dve.tensor_copy(wgT[:], g_ps.rearrange("p (k e) -> p k e", k=KD)).then_inc(small_copied, 1)
            dve.tensor_copy(a_sb[:, :, :, KEYS:KG], g_ps.rearrange("p (k o e) -> p k o e", k=KD, o=1).to_broadcast([P, KD, B, E])).then_inc(small_copied, 1)
            dve.wait_ge(prep_pe, 5)
            dve.tensor_copy(a_raw[:], bank[5][:].rearrange("p (k i) -> p k i", k=KD)).then_inc(a_copied, 1)
            dve.wait_ge(prep_pe, 6)
            dve.tensor_copy(c_sb[:], bank[6][:, 0:B * KEYS]).then_inc(c_copied, 1)
            dve.wait_ge(prep_pe, 7)
            dve.wait_ge(a_copied, 1)
            for k in range(KD):
                dve.tensor_tensor(a_sb[:, k, :, 0:KEYS], a_raw[:, k].rearrange("p (b i) -> p b i", b=B), bank[7][:, 0:B * KEYS].rearrange("p (b i) -> p b i", b=B), ALU.subtract).then_inc(a_centred, 1)
            dve.wait_ge(prep_pe, 8)
            dve.tensor_copy(wvT[:], bank[3][:, 0:KD * CD].rearrange("p (k i) -> p k i", k=KD)).then_inc(wvT_copied, 1)
            dve.wait_ge(wv_in, 64)
            for k in range(KD):
                dve.tensor_scalar(bv_wide[:, k, :], ones[:], bv_col[:, k:k + 1], None, ALU.mult).then_inc(bv_wide_made, 1)

            def value_gates():
                dve.wait_ge(prep_pe, 9)
                dve.tensor_copy(wv_sb[:, 0, D:ROW], bank[4][:, 0:E]).then_inc(vg_copied, 1)
                dve.tensor_copy(wv_sb[0:CR, 1, D:ROW], bank[4][0:CR, E:2 * E]).then_inc(vg_copied, 1)
                dve.tensor_copy(bv_sb[:, D:ROW], bank[4][:, 2 * E:3 * E]).then_inc(vg_copied, 1)

            def values(b):
                dve.wait_ge(prep_pe, 10 + b)
                dve.wait_ge(vg_copied, 3)
                dve.wait_ge(values_zeroed, 1)
                for t in range(2):
                    half = slice(t * KEYS, (t + 1) * KEYS)
                    dve.tensor_tensor(v_sb[half, b, t], bank[5 + b % 3][half, 0:ROW], bv_sb[half], ALU.add).then_inc(values_made, 1)

            n = 0

            def then(ins, meanwhile=lambda: None):
                nonlocal n
                n += 1
                ins.then_inc(route, 1)
                meanwhile()
                dve.wait_ge(route, n)

            def choose(k, t0, t1, meanwhile=lambda step: None):
                def wide(ap):
                    return ap.rearrange("p (t o) -> p t o", o=1).to_broadcast([P, t1 - t0, E])

                left = (gates, rest)[k][:, t0:t1]
                some = same[:, t0:t1]
                then(dve.tensor_reduce(best[:, k, t0:t1], left, AX.X, ALU.max), lambda: meanwhile(0))
                then(dve.tensor_tensor(some, left, wide(best[:, k, t0:t1]), ALU.is_equal), lambda: meanwhile(1))
                then(dve.tensor_tensor(some, some, iota_e8[:, t0:t1], ALU.mult), lambda: meanwhile(2))
                then(dve.tensor_reduce(choice[:, k, t0:t1], some, AX.X, ALU.min))
                then(dve.tensor_tensor(hot[:, k, t0:t1], iota_e8[:, t0:t1], wide(choice[:, k, t0:t1]), ALU.is_equal))
                if k == 0:
                    then(dve.scalar_tensor_tensor(out=rest[:, t0:t1], in0=hot[:, 0, t0:t1], scalar=-2.0, in1=gates[:, t0:t1], op0=ALU.mult, op1=ALU.add))

            def slots(t0, t1, meanwhile=lambda step: None):
                late = t0 > 0
                total, prefix = count_cols(ps_total, late), count_cols(ps_prefix, late)
                (run, n_run), (keep, _) = scan_rows(running)[late], scan_rows(scan_keep)[late]
                dve.wait_ge(counts_made, late + 1)
                if late:
                    dve.tensor_copy(late_total[:, :, 0], scan_rows(running)[0][0][:, :, EARLY - 1])
                    then(dve.tensor_copy(late_total[:, :, 1:], total.rearrange("p (m t) -> p m t", m=CHOICES)))
                    total = late_total[:].rearrange("p m t -> p (m t)")
                then(dve.tensor_tensor_scan(run.rearrange("p m t -> p (m t)"), keep.rearrange("p m t -> p (m t)"), total, 0.0, ALU.mult, ALU.add), lambda: meanwhile(0))
                then(dve.tensor_tensor(place[:, :, t0:t1], run[:, :, n_run - (t1 - t0):], prefix.rearrange("p (m t) -> p m t", m=CHOICES), ALU.add), lambda: meanwhile(1))
                for k in range(TOP_K):
                    ins = dve.tensor_tensor(picked[:, k * E:(k + 1) * E, t0:t1], place[:, k * E:(k + 1) * E, t0:t1], hot[:, k, t0:t1].rearrange("p t e -> p e t"), ALU.mult)
                then(ins, lambda: meanwhile(2))
                for k in range(TOP_K):
                    ins = dve.tensor_reduce(count[:, k, t0:t1], picked[:, k * E:(k + 1) * E, t0:t1].rearrange("p e t -> p t e"), AX.X, ALU.add)
                then(ins)
                cut = slice(t0, t1)
                dve.tensor_scalar(over[:, :, cut], count[:, :, cut], float(C), 4.0 * NT, ALU.is_ge, ALU.mult)
                dve.scalar_tensor_tensor(out=slot[:, 0, cut], in0=choice[:, 0, cut], scalar=float(SLOTS), in1=count[:, 0, cut], op0=ALU.mult, op1=ALU.add)
                then(dve.scalar_tensor_tensor(out=slot[:, 1, cut], in0=choice[:, 1, cut], scalar=float(SLOTS), in1=count[:, 1, cut], op0=ALU.mult, op1=ALU.subtract))
                dve.tensor_scalar(slot[:, 0, cut], slot[:, 0, cut], float(SLOTS * E), None, ALU.add)
                then(dve.tensor_scalar(slot[:, 1, cut], slot[:, 1, cut], float(SLOTS * E + C - 1), None, ALU.add))
                then(dve.tensor_scalar(tile_f[:, :, cut], slot[:, :, cut], -(P - 1) / 2.0, 1.0 / P, ALU.add, ALU.mult))
                then(dve.tensor_scalar(tile_f[:, :, cut], tile_f[:, :, cut], ROUNDER, -ROUNDER, ALU.add, ALU.add))
                dve.scalar_tensor_tensor(out=slot_lo[:, :, cut], in0=tile_f[:, :, cut], scalar=-float(P), in1=slot[:, :, cut], op0=ALU.mult, op1=ALU.add)
                then(dve.tensor_tensor(tile_of[:, :, cut], tile_f[:, :, cut], over[:, :, cut], ALU.add))

            def of_chunk(row, chunk, size):
                return row[:, CH * chunk:CH * (chunk + 1)].rearrange("p (o n) -> p o n", o=1).to_broadcast([P, size, CH])

            def tile_ones(chunk, k):
                dve.wait_ge(hot_free, 2 * chunk + k + 1)
                dve.tensor_tensor(tile_hot[:, k], iota_tile[:], of_chunk(tile_of[:, k], chunk, NT), ALU.is_equal).then_inc(tile_hot_made, 1)

            def slot_ones(chunk, k):
                dve.tensor_tensor(slot_hot[:, k], iota_slot[:], of_chunk(slot_lo[:, k], chunk, P), ALU.is_equal)

            def tile_numbers(chunk, k):
                dve.wait_ge(tile_hot_made, 2 * chunk + k + 1)
                dve.tensor_tensor(tokens_hot[:, k, 1], tile_hot[:, k], of_chunk(tile_no, chunk, NT), ALU.mult).then_inc(hot_made, 1)

            def one_hots(chunk, k):
                tile_ones(chunk, k)
                slot_ones(chunk, k)
                tile_numbers(chunk, k)

            def step1(it, j, on):
                pair = 4 * it + j
                if on[3]:
                    r, ring = (j - 3) % 2, (j - 3) % 4
                    dve.wait_ge(att_made, pair - 2)
                    dve.wait_ge(xg_copied, pair - 2)
                    dve.wait_ge(pinv_made, pair - 2)
                    dve.wait_ge(x1_stored[r], 16 * (2 * it + (j - 3) // 2 + 1))
                    dve.wait_ge(rows0_made, upto(pair - 3))
                    dve.wait_ge(rows1_made, upto(pair - 3))
                    for t in range(2):
                        ins = dve.scalar_tensor_tensor(out=x1[:, r, t], in0=ps_att[t][:, 0:ROW], scalar=pinv[:, r, t:t + 1],
                                                       in1=x_sb[:, ring, t], op0=ALU.mult, op1=ALU.add)
                    ins.then_inc(x1_made, 1)
                if on[2]:
                    r = j % 2
                    dve.wait_ge(probs_made, upto(pair - 1))
                    dve.reciprocal(pinv[:, r], psum_row[:, r]).then_inc(pinv_made, 1)
                if on[1]:
                    r, start = (j - 1) % 2, KEYS * it + KEYS * ((j - 1) // 4)
                    dve.wait_ge(scores_made, pair)
                    dve.wait_ge(rstd1_made, pair)
                    dve.wait_ge(probs_made, upto(pair - 2))
                    for t in range(2):
                        ins = dve.scalar_tensor_tensor(out=score[:, r, t], in0=ps_score[:, t * KG:t * KG + KEYS], scalar=rstd1[:, r, t:t + 1],
                                                       in1=cols(c_sb, start, KEYS), op0=ALU.mult, op1=ALU.add)
                    ins.then_inc(scores_read, 1)
                if on[0]:
                    r, ring = j % 2, j % 4
                    dve.wait_ge(x_in[ring], 16 * (it + 1))
                    for t in range(2):
                        ins = dve.bn_stats(stat1[:, r, t], x_sb[:, ring, t, 0:D])
                    ins.then_inc(stats1_made, 1)
                if on[3]:
                    r = (j - 3) % 2
                    dve.wait_ge(x1_made, pair - 2)
                    for t in range(2):
                        ins = dve.bn_stats(stat2[:, r, t], x1[:, r, t, 0:D])
                    ins.then_inc(stats2_made, 1)
                if on[1]:
                    r = (j - 1) % 2
                    dve.wait_ge(scores_read, pair)
                    dve.tensor_reduce(nmax[:, r], score[:, r], AX.X, ALU.max, negate=True).then_inc(score_scaled, 1)
                if gates_due(it, j):
                    r, batch = j // 2, gate_batch(it, j)
                    logits = rows[:, j - 1:j + 1, :, D:ROW].rearrange("p n t e -> p (n t) e")
                    dve.wait_ge(rows0_made, pair - 2)
                    dve.wait_ge(rows1_made, pair - 2)
                    dve.tensor_reduce(gmax[:, r], logits, AX.X, ALU.max).then_inc(gmax_made, 1)
                if on[0]:
                    r = j % 2
                    dve.wait_ge(stats1_made, pair + 1)
                    dve.wait_ge(var1_made, upto(pair - 1))
                    dve.sem_inc(dve_waits, 1)
                    for t in range(2):
                        ins = dve.bn_aggr(mv1[:, r, t], stat1[:, r, t])
                    ins.then_inc(mv1_made, 1)
                if gates_due(it, j):
                    r = j // 2
                    dve.wait_ge(gmax_made, batch)
                    dve.tensor_tensor(gsub[:, r], logits, gmax[:, r].rearrange("p (t o) -> p t o", o=1).to_broadcast([P, 4, E]), ALU.subtract).then_inc(gsub_made, 1)
                if on[3]:
                    r = (j - 3) % 2
                    dve.wait_ge(stats2_made, pair - 2)
                    dve.sem_inc(dve_waits, 1)
                    for t in range(2):
                        ins = dve.bn_aggr(mv2[:, r, t], stat2[:, r, t])
                    ins.then_inc(mv2_made, 1)
                if gates_due(it, j):
                    r = j // 2
                    dve.wait_ge(gexp_made, batch)
                    dve.tensor_reduce(gsum[:, r], gexp[:, r], AX.X, ALU.add).then_inc(gsum_made, 1)
                    dve.wait_ge(gsum_made, batch)
                    dve.reciprocal(ginv[:, r], gsum[:, r]).then_inc(ginv_made, 1)
                    dve.wait_ge(ginv_made, batch)
                    first = 4 * (batch - 1)
                    to = gates[:, first:first + 4, :] if isinstance(it, int) else gates[:, bass.ds(first, 4), :]
                    inv = ginv[:, r].rearrange("p (t o) -> p t o", o=1).to_broadcast([P, 4, E])
                    dve.tensor_tensor(rows[:, j - 1:j + 1, :, D:ROW].rearrange("p n t e -> p (n t) e"), gexp[:, r], inv, ALU.mult).then_inc(rows_gated, 1)
                    dve.tensor_tensor(to, gexp[:, r], inv, ALU.mult).then_inc(gates_made, 1)
                if isinstance(it, int) and it == 0:
                    if j == 0:
                        value_gates()
                    for b in value_batches[j]:
                        values(b)
                if isinstance(it, int) and it == PAIRS // PB and j < 2:
                    if j == 0:
                        dve.wait_ge(gates_made, EARLY // 4)
                    choose(j, 0, EARLY)
                if isinstance(it, int) and it == PAIRS // PB and j == 2:
                    routed.append(n)
                    slots(0, EARLY)
                    for k in range(TOP_K):
                        one_hots(0, k)

            steps_of_part1(dve, step1)

            dve.wait_ge(gates_made, PAIRS // 2)
            for k in range(TOP_K):
                choose(k, EARLY, TILES, lambda step: (tile_ones, slot_ones, tile_numbers)[step](1, k))
            routed.append(n)
            one_hots(2, 0)
            slots(EARLY, TILES, lambda step: (tile_ones, slot_ones, tile_numbers)[step](2, 1))
            for k in range(TOP_K):
                one_hots(3, k)

            dve.wait_ge(table_made, 1)
            then(dve.tensor_copy(table[:].rearrange("p k a c -> p (k a c)"), ps_table[:, 0:4 * NT]))
            then(dve.scalar_tensor_tensor(out=table0[:], in0=table[:, :, 1], scalar=float(P), in1=table[:, :, 0], op0=ALU.mult, op1=ALU.add))
            then(dve.scalar_tensor_tensor(out=table1[:], in0=table0[:, 0], scalar=0.0, in1=table0[:, 1], op0=ALU.is_equal, op1=ALU.mult))
            then(dve.tensor_tensor(table1[:], table1[:], table0[:, 0], ALU.add))
            then(dve.scalar_tensor_tensor(out=table2[:], in0=table1[:], scalar=0.0, in1=trash[:], op0=ALU.is_equal, op1=ALU.mult))
            dve.scalar_tensor_tensor(out=slot_token[:], in0=table1[:], scalar=-1.0, in1=table2[:], op0=ALU.add, op1=ALU.add).then_inc(slots_ready, 1)

            def input_low(it, u):
                unit, N, ring = BODY * it + u, unit_cols(u), u % 3
                e = 2 * it + u // UE
                for k in range(KD):
                    dve.wait_ge(in_hi_made, KD * unit + k + 1)
                    dve.tensor_tensor(in_lo[u % 2][:, k, 0:N], ps_turn[k][:, 0:N], in_hi[u % 2][:, k, 0:N].bitcast(F32), ALU.subtract).then_inc(in_lo_made, 1)
                gate = gathered[:, ring, :, D + e:D + e + 1] if isinstance(e, int) else gathered[:, ring, :, bass.ds(D + e, 1)]
                dve.wait_ge(y_ready, upto(UT * (unit - 2) + 1))
                dve.tensor_copy(gate_of[:, ring], gate.rearrange("p j o -> p (j o)")).then_inc(gate_copied, 1)

            def hidden_parts(it, u, halfway=None):
                unit, N = BODY * it + u, unit_cols(u)
                dve.wait_ge(down_made, upto(UT * (unit - 1) + 1))

                def low(c):
                    chunk = HC * u + c
                    dve.wait_ge(h_hi_made, HC * unit + c + 1)
                    dve.tensor_tensor(h_lo[u % 2][:, c, 0:N], h_f32[:, chunk % 3, 0:N], h_hi[u % 2][:, c, 0:N].bitcast(F32), ALU.subtract).then_inc(h_lo_made, 1)

                for c in range(HC):
                    chunk = HC * u + c
                    if halfway and c == HC // 2:
                        halfway()
                    dve.wait_ge(gelu_made, HC * unit + c + 1)
                    dve.tensor_copy(h_hi[u % 2][:, c, 0:N], h_f32[:, chunk % 3, 0:N]).then_inc(h_hi_made, 1)
                    if c:
                        low(c - 1)
                low(HC - 1)

            input_low(0, 0)
            hidden_parts(0, 0, halfway=lambda: input_low(0, 1))

            def step3(it, u, last):
                unit, par = BODY * it + u, (u // UE) % 2
                if not last or u + 1 < BODY:
                    hidden_parts(it, u + 1)
                if not last or u + 2 < BODY:
                    input_low(it, u + 2)
                if u % UE == 0:
                    dve.wait_ge(b2_in[par], 16 * (it + 1))
                dve.wait_ge(y_added, 16 * (UT * unit + 1))
                for j in range(UT):
                    m, tile = tile_rows(u, j), UT * unit + j
                    dve.wait_ge(down_made, tile + 2)
                    dve.tensor_tensor(y_sum[0:m, j], ps_y[j][0:m, 0:D], b2_wide[0:m, par], ALU.add).then_inc(y_summed, 1)
                    dve.wait_ge(y_summed, tile + 2)
                    dve.tensor_scalar(y_out[0:m, j], y_sum[0:m, j], gate_of[0:m, u % 3, j:j + 1], None, ALU.mult).then_inc(y_ready, 1)

            steps_of_part3(dve, step3)

        @block.tensor
        def _(pe):

            for begun in (up_made, down_made):
                pe.sem_inc(begun, 1)
            pe.sem_inc(hot_free, 2)

            pe.wait_ge(ctx_in, 16)
            pe.wait_ge(consts, 1)
            for n in range(2):
                pe.transpose(bank[0][:, n * P:(n + 1) * P], ctx_sb[:, n, 0:P], ident[:])
                ins = pe.transpose(bank[0][0:CR, B * KEYS + n * P:B * KEYS + (n + 1) * P], ctx_sb[:, n, P:CD], ident[:])
            ins.then_inc(prep_pe, 1)
            pe.wait_ge(wq_in, 16)
            for i in range(KD):
                for h in range(KD):
                    ins = pe.transpose(bank[1][:, h * D + i * P:h * D + (i + 1) * P], wq_sb[:, i, h * P:(h + 1) * P], ident[:])
            ins.then_inc(prep_pe, 1)
            pe.wait_ge(wk_in, 48)
            pe.wait_ge(ctxT_copied, 2)
            for h in range(KD):
                to = bank[2][:, h * D:h * D + B * KEYS]
                pe.matmul(to, wk_sb[:, 0, h * P:(h + 1) * P], ctxT[:, 0, :], start=True, stop=False)
                ins = pe.matmul(to, wk_sb[0:CR, 1, h * P:(h + 1) * P], ctxT[0:CR, 1, :], start=False, stop=True)
            ins.then_inc(prep_pe, 1)
            pe.wait_ge(b1_in, 16)
            pe.wait_ge(wg_centred, 3)
            pe.transpose(bank[0][:, 0:E * HC], b1_sb[:], ident[0:E * HC, 0:E * HC])
            for k in range(KD):
                ins = pe.transpose(bank[0][:, E * HC + k * E:E * HC + (k + 1) * E], wg_mid[:, k * P:(k + 1) * P], ident[0:E, 0:E])
            ins.then_inc(prep_pe, 1)
            pe.wait_ge(wqT_copied, 1)
            pe.wait_ge(key_made, KD)
            for i in range(KD):
                for h in range(KD):
                    ins = pe.matmul(bank[5][:, i * D:(i + 1) * D], wqT[:, h, i * P:(i + 1) * P], keyT[:, h, :], start=(h == 0), stop=(h == KD - 1))
            ins.then_inc(prep_pe, 1)
            pe.wait_ge(bq_wide_made, KD)
            for h in range(KD):
                ins = pe.matmul(bank[6][:, 0:B * KEYS], bq_wide[:, h, :], keyT[:, h, :], start=(h == 0), stop=(h == KD - 1))
            ins.then_inc(prep_pe, 1)
            pe.wait_ge(a_copied, 1)
            for k in range(KD):
                ins = pe.matmul(bank[7][:, 0:B * KEYS], mean_w[:], a_raw[:, k, :], start=(k == 0), stop=(k == KD - 1))
            ins.then_inc(prep_pe, 1)
            pe.wait_ge(wv_in, 64)
            for h in range(KD):
                pe.transpose(bank[3][:, h * CD:h * CD + P], wv_sb[:, 0, h * P:(h + 1) * P], ident[:])
                ins = pe.transpose(bank[3][:, h * CD + P:(h + 1) * CD], wv_sb[0:CR, 1, h * P:(h + 1) * P], ident[0:CR, 0:CR])
            ins.then_inc(prep_pe, 1)

            def value_gates():
                pe.wait_ge(wvT_copied, 1)
                pe.wait_ge(bv_wide_made, KD)
                for h in range(KD):
                    pe.matmul(bank[4][:, 0:E], wvT[:, h, 0:P], wgT[:, h, :], start=(h == 0), stop=(h == KD - 1))
                for h in range(KD):
                    pe.matmul(bank[4][0:CR, E:2 * E], wvT[:, h, P:CD], wgT[:, h, :], start=(h == 0), stop=(h == KD - 1))
                for h in range(KD):
                    ins = pe.matmul(bank[4][:, 2 * E:3 * E], bv_wide[:, h, :], wgT[:, h, :], start=(h == 0), stop=(h == KD - 1))
                ins.then_inc(prep_pe, 1)

            def values(b):
                if b == 0:
                    pe.wait_ge(vg_copied, 3)
                    pe.wait_ge(ctxT_doubled, 2)
                    pe.wait_ge(c_copied, 1)
                    pe.wait_ge(a_centred, KD)
                if b == 3:
                    pe.wait_ge(values_made, 2)
                to = bank[5 + b % 3][:, 0:ROW]
                pe.matmul(to, ctxT_twice[:, 0, b].rearrange("p o k -> p (o k)"), wv_sb[:, 0, :], start=True, stop=False)
                pe.matmul(to, ctxT_twice[0:CR, 1, b].rearrange("p o k -> p (o k)"), wv_sb[0:CR, 1, :], start=False, stop=True).then_inc(prep_pe, 1)

            def step1(it, j, on):
                pair = 4 * it + j
                if on[1]:
                    r, start = (j - 1) % 2, KG * it + KG * ((j - 1) // 4)
                    if isinstance(it, int) and it == 0 and j == 1:
                        pe.wait_ge(a_centred, KD)
                    pe.wait_ge(xT_copied, pair)
                    pe.wait_ge(scores_read, upto(pair - 1))
                    pe.wait_ge(xg_copied, upto(pair - 1))
                    for t in range(2):
                        for k in range(KD):
                            ins = pe.matmul(ps_score[:, t * KG:(t + 1) * KG], xT[:, r, k, t * P:(t + 1) * P],
                                            cols(a_sb[:, k].rearrange("p b c -> p (b c)"), start, KG), start=(k == 0), stop=(k == KD - 1))
                    ins.then_inc(scores_made, 1)
                if on[2]:
                    r = j % 2
                    pe.wait_ge(probs_made, upto(pair - 1))
                    pe.wait_ge(pT_copied, upto(pair - 2))
                    pe.sem_inc(pe_waits, 1)
                    pe.transpose(ps_pT[:, 0:P], prob[:, r].rearrange("p t k -> p (t k)"), ident[:]).then_inc(pT_made, 1)
                if on[0]:
                    pe.wait_ge(x_in[j % 4], 16 * (it + 1))
                    pe.wait_ge(xT_copied, pair)
                    for k in range(KD):
                        for t in range(2):
                            at = k * 2 * P + t * P
                            ins = pe.transpose(ps_xT[:, at:at + P], x_sb[:, j % 4, t, k * P:(k + 1) * P], ident[:])
                    ins.then_inc(xT_made, 1)
                    if isinstance(it, int) and it == 0 and j == 0:
                        value_gates()
                if on[2]:
                    r = j % 2
                    batch = it + (j - 2) // 4
                    v = v_sb[:, batch] if isinstance(batch, int) else v_sb[:, bass.ds(batch, 1)].rearrange("p o t d -> p (o t) d")
                    if j == 2:
                        pe.wait_ge(values_made, 2 if isinstance(it, int) else 2 * B)
                    pe.wait_ge(pT_copied, upto(pair - 1))
                    pe.wait_ge(x1_made, upto(pair - 2))
                    pe.sem_inc(pe_waits, 1)
                    for t in range(2):
                        ins = pe.matmul(ps_att[t][:, 0:ROW], pT[:, r, :], v[:, t], start=True, stop=True)
                    ins.then_inc(att_made, 1)
                if isinstance(it, int) and it == 0:
                    for b in value_batches[j]:
                        values(b)

            pe.wait_ge(small_copied, 3)
            steps_of_part1(pe, step1)

            def counts(t0, t1):
                late = t0 > 0
                pe.wait_ge(route, routed[late])
                for k in range(TOP_K):
                    half = slice(k * E * (t1 - t0), (k + 1) * E * (t1 - t0))
                    moving = hot[:, k, t0:t1].rearrange("p t e -> p e t")
                    pe.matmul(count_cols(ps_total, late)[:, half], ones_bf[:], moving, start=True, stop=True)
                    ins = pe.matmul(count_cols(ps_prefix, late)[:, half], before[:], moving, start=True, stop=True)
                ins.then_inc(counts_made, 1)

            def add_to_table(chunk, k):
                tokens = tokens_hot[:, k].rearrange("p a c n -> p n (a c)")
                pe.wait_ge(hot_made, 2 * chunk + k + 1)
                pe.wait_ge(token_rows_made, 2 * chunk + k + 1)
                for n in range(CH):
                    ins = pe.matmul(ps_table[:, 2 * k * NT:2 * (k + 1) * NT], slot_hot[:, k, :, n], tokens[:, n], start=False, stop=False, skip_group_check=True)
                ins.then_inc(hot_free, 1)

            counts(0, EARLY)
            pe.matmul(ps_table[:, 0:4 * NT], zeros_bf[:, 0:P], zeros_bf[:], start=True, stop=False, skip_group_check=True)
            for k in range(TOP_K):
                add_to_table(0, k)
            for k in range(TOP_K):
                add_to_table(1, k)
            counts(EARLY, TILES)
            for chunk in range(2, TILES // CH):
                for k in range(TOP_K):
                    add_to_table(chunk, k)
            pe.matmul(ps_table[:, 0:4 * NT], zeros_bf[:, 0:P], zeros_bf[:], start=False, stop=True, skip_group_check=True).then_inc(table_made, 1)

            def turn(it, u):
                unit, ring = BODY * it + u, u % 3
                pe.wait_ge(rows_in[ring], 16 * UT * (2 * it + u // 3 + 1))
                pe.wait_ge(in_lo_made, KD * unit)
                for k in range(KD):
                    for j in range(UT):
                        m = tile_rows(u, j)
                        ins = pe.transpose(ps_turn[k][:, j * P:j * P + m], gathered[0:m, ring, j, k * P:(k + 1) * P], ident[0:m, 0:m])
                ins.then_inc(turned, 1)

            def up(it, u, halfway=None):
                unit, N, e, par = BODY * it + u, unit_cols(u), 2 * it + u // UE, (u // UE) % 2
                if u % UE == 0:
                    pe.wait_ge(w1_hi_made, 4 * e + 4)
                    pe.wait_ge(w1_lo_made, 4 * e + 4)
                for c in range(HC):
                    chunk, cut = HC * u + c, slice(c * P, (c + 1) * P)
                    to = ps_up[chunk % 3][:, 0:N]
                    if halfway and c == HC // 2:
                        halfway()
                    pe.wait_ge(gelu_made, upto(HC * unit + c - 2))
                    for k in range(KD):
                        hi, lo = in_hi[u % 2][:, k, 0:N], in_lo[u % 2][:, k, 0:N]
                        if c == 0:
                            pe.wait_ge(in_hi_made, KD * unit + k + 1)
                        pe.matmul(to, w1_hi[par][:, k, cut], hi, start=(k == 0), stop=False)
                        pe.matmul(to, w1_lo[par][:, k, cut], hi, start=False, stop=False)
                        if c == 0:
                            pe.wait_ge(in_lo_made, KD * unit + k + 1)
                        ins = pe.matmul(to, w1_hi[par][:, k, cut], lo, start=False, stop=(k == KD - 1))
                    ins.then_inc(up_made, 1)

            def down(it, u):
                unit, e, par = BODY * it + u, 2 * it + u // UE, (u // UE) % 2
                pe.wait_ge(y_summed, UT * unit + 1)
                if u % UE == 0:
                    pe.wait_ge(w2_hi_made, 4 * e + 4)
                    pe.wait_ge(w2_lo_made, 4 * e + 4)
                for j in range(UT):
                    m = tile_rows(u, j)
                    to = ps_y[j][0:m, 0:D]
                    for c in range(HC):
                        if j == 0:
                            pe.wait_ge(h_lo_made, HC * unit + c + 1)
                        hi, lo = (h[u % 2][:, c, j * P:j * P + m] for h in (h_hi, h_lo))
                        pe.matmul(to, hi, w2_hi[par][:, c, :], start=(c == 0), stop=False)
                        pe.matmul(to, hi, w2_lo[par][:, c, :], start=False, stop=False)
                        ins = pe.matmul(to, lo, w2_hi[par][:, c, :], start=False, stop=(c == HC - 1))
                    ins.then_inc(down_made, 1)

            turn(0, 0)
            up(0, 0, halfway=lambda: turn(0, 1))

            def step3(it, u, last):
                if not last or u + 1 < BODY:
                    up(it, u + 1)
                if not last or u + 2 < BODY:
                    turn(it, u + 2)
                down(it, u)

            steps_of_part3(pe, step3)


_INS = ["x", "ctx_768", "L0_xattn_Wq", "L0_xattn_bq", "L0_xattn_Wk", "L0_xattn_bk", "L0_xattn_Wv", "L0_xattn_bv",
        "L0_ffn_Wg", "L0_ffn_W1", "L0_ffn_b1", "L0_ffn_W2", "L0_ffn_b2"]


def kernel(**inputs):
    import numpy as _np
    import concourse.bacc as _bacc
    from concourse import mybir as _mybir
    from concourse.bass_utils import run_bass_kernel_spmd as _run

    nc = _bacc.Bacc("TRN2", target_bir_lowering=False, num_devices=1)
    arrays, args = {}, []
    for name in _INS:
        a = _np.ascontiguousarray(inputs[name])
        arrays[f"in_{name}_dram"] = a
        args.append(nc.dram_tensor(f"in_{name}_dram", a.shape, _mybir.dt.from_np(a.dtype), kind="ExternalInput").ap())
    B, S, D = inputs["x"].shape
    args.append(nc.dram_tensor("out_0_dram", (B * S + P, D), _mybir.dt.float32, kind="ExternalOutput").ap())
    xattn_moe(nc, *args)
    r = _run(nc, [arrays], core_ids=[0])
    return r.results[0]["out_0_dram"][:B * S].reshape(B, S, D)
```
